# Optimizing a Trainium2 kernel written in Bass

```python
import numpy as np
import jax
import jax.numpy as jnp

def _softmax(x, axis=-1):
    return jax.nn.softmax(x, axis=axis)

def _gelu(x):
    return jax.nn.gelu(x, approximate=True)

def _silu(x):
    return jax.nn.silu(x)

def _sigmoid(x):
    return jax.nn.sigmoid(x)

def _layernorm(x, axis=-1, eps=1e-05):
    m = jnp.mean(x, axis=axis, keepdims=True)
    v = jnp.var(x, axis=axis, keepdims=True)
    return (x - m) / jnp.sqrt(v + eps)

def _scatter_add(tgt, idx, src, axis=0):
    return tgt.at[idx].add(src)

def _segment_sum(src, seg, n):
    return jax.ops.segment_sum(src, seg, n)
kernel_name = 'mk_adj_preln_d2_adj_r2_8d4df4'

def setup_inputs(seed: int=0):
    np.random.seed(seed)
    _w = jnp.asarray

    def _rec_inputs():
        import jax
        import jax.numpy as jnp
        _gk = jax.random.key(seed)
        x = -0.001547 + 1.001 * jax.random.normal(jax.random.fold_in(_gk, 1), (64, 128, 128), jnp.float32)
        _a = jax.random.bernoulli(jax.random.fold_in(_gk, 2), 0.03125, (64, 128, 128))
        _a = jnp.logical_or(_a, jnp.eye(128, dtype=bool))
        adj = _a.astype(jnp.int32)
        _nm = jnp.ones((64, 128), dtype=bool)
        nodemask = jnp.where(_nm, 1.0, 0.0).astype(jnp.float32)
        return (x, adj, nodemask)
    x, adj, nodemask = _rec_inputs()

    def _L0_gnn_setup():
        import jax, jax.numpy as jnp
        import numpy as np
        D_MODEL = 128
        NUM_REL = 40

        def _direction(x, W, Wg, b, bg, adj, rel_ids):
            h = x @ W.T
            g = h @ Wg.T
            vals = (h[:, :, None, :] + b) * jax.nn.sigmoid(g[:, :, None, :] + bg)
            onehot = (adj[..., None] == rel_ids).astype(h.dtype)
            return jnp.einsum('bnmr,bmrd->bnd', onehot, vals)
        key = jax.random.key(seed)
        ks = jax.random.split(key, 16)
        B, N, d = (2, 256, D_MODEL)
        s = 0.02
        inp = {'node': jax.random.normal(ks[0], (B, N, d), dtype=jnp.float32), 'node_mask': jnp.ones((B, N), dtype=jnp.float32), 'adj_mat': jax.random.randint(ks[1], (B, N, N), 0, 41, dtype=jnp.int32), 'W_fwd': jax.random.normal(ks[2], (d, d), dtype=jnp.float32) * s, 'W_bwd': jax.random.normal(ks[3], (d, d), dtype=jnp.float32) * s, 'W_loop': jax.random.normal(ks[4], (d, d), dtype=jnp.float32) * s, 'Wg_fwd': jax.random.normal(ks[5], (d, d), dtype=jnp.float32) * s, 'Wg_bwd': jax.random.normal(ks[6], (d, d), dtype=jnp.float32) * s, 'Wg_loop': jax.random.normal(ks[7], (d, d), dtype=jnp.float32) * s, 'b_fwd': jax.random.normal(ks[8], (NUM_REL - 1, d), dtype=jnp.float32) * s, 'b_bwd': jax.random.normal(ks[9], (NUM_REL - 1, d), dtype=jnp.float32) * s, 'b_loop': jax.random.normal(ks[10], (1, d), dtype=jnp.float32) * s, 'bg_fwd': jax.random.normal(ks[11], (NUM_REL - 1, d), dtype=jnp.float32) * s, 'bg_bwd': jax.random.normal(ks[12], (NUM_REL - 1, d), dtype=jnp.float32) * s, 'bg_loop': jax.random.normal(ks[13], (1, d), dtype=jnp.float32) * s}
        return inp
    _L0_gnn_all = _L0_gnn_setup()
    _L0_gnn_in = {k: v for k, v in _L0_gnn_all.items() if k in ('W_fwd', 'W_bwd', 'W_loop', 'Wg_fwd', 'Wg_bwd', 'Wg_loop', 'b_fwd', 'b_bwd', 'b_loop', 'bg_fwd', 'bg_bwd', 'bg_loop')}
    del _L0_gnn_all

    def _L1_gnn_setup():
        import jax, jax.numpy as jnp
        import numpy as np
        D = 128
        B, N = (16, 512)
        NEG_SLOPE = 0.2
        SCALE = float(np.sqrt(D))
        key = jax.random.key(seed)
        ks = jax.random.split(key, 8)
        s = 1.0 / np.sqrt(D)
        return {'feature': jax.random.normal(ks[0], (B, N, D), dtype=jnp.float32), 'graph': jax.random.randint(ks[1], (B, N, N), 0, 2, dtype=jnp.int32), 'W_w': jax.random.uniform(ks[2], (D, D), jnp.float32, -s, s), 'W_b': jax.random.uniform(ks[3], (D,), jnp.float32, -s, s), 'Q_w': jax.random.uniform(ks[4], (D, D), jnp.float32, -s, s), 'Q_b': jax.random.uniform(ks[5], (D,), jnp.float32, -s, s), 'K_w': jax.random.uniform(ks[6], (D, D), jnp.float32, -s, s), 'K_b': jax.random.uniform(ks[7], (D,), jnp.float32, -s, s)}
    _L1_gnn_all = _L1_gnn_setup()
    _L1_gnn_in = {k: v for k, v in _L1_gnn_all.items() if k in ('W_w', 'W_b', 'Q_w', 'Q_b', 'K_w', 'K_b')}
    del _L1_gnn_all
    return {'x': x, 'adj': adj, 'nodemask': nodemask, 'L0_gnn_W_fwd': _L0_gnn_in['W_fwd'], 'L0_gnn_W_bwd': _L0_gnn_in['W_bwd'], 'L0_gnn_W_loop': _L0_gnn_in['W_loop'], 'L0_gnn_Wg_fwd': _L0_gnn_in['Wg_fwd'], 'L0_gnn_Wg_bwd': _L0_gnn_in['Wg_bwd'], 'L0_gnn_Wg_loop': _L0_gnn_in['Wg_loop'], 'L0_gnn_b_fwd': _L0_gnn_in['b_fwd'], 'L0_gnn_b_bwd': _L0_gnn_in['b_bwd'], 'L0_gnn_b_loop': _L0_gnn_in['b_loop'], 'L0_gnn_bg_fwd': _L0_gnn_in['bg_fwd'], 'L0_gnn_bg_bwd': _L0_gnn_in['bg_bwd'], 'L0_gnn_bg_loop': _L0_gnn_in['bg_loop'], 'L1_gnn_W_w': _L1_gnn_in['W_w'], 'L1_gnn_W_b': _L1_gnn_in['W_b'], 'L1_gnn_Q_w': _L1_gnn_in['Q_w'], 'L1_gnn_Q_b': _L1_gnn_in['Q_b'], 'L1_gnn_K_w': _L1_gnn_in['K_w'], 'L1_gnn_K_b': _L1_gnn_in['K_b']}

def reference(x, adj, nodemask, L0_gnn_W_fwd, L0_gnn_W_bwd, L0_gnn_W_loop, L0_gnn_Wg_fwd, L0_gnn_Wg_bwd, L0_gnn_Wg_loop, L0_gnn_b_fwd, L0_gnn_b_bwd, L0_gnn_b_loop, L0_gnn_bg_fwd, L0_gnn_bg_bwd, L0_gnn_bg_loop, L1_gnn_W_w, L1_gnn_W_b, L1_gnn_Q_w, L1_gnn_Q_b, L1_gnn_K_w, L1_gnn_K_b):
    import jax
    import jax.numpy as jnp

    def _L0_gnn_ref(node, node_mask, adj_mat, W_fwd, W_bwd, W_loop, Wg_fwd, Wg_bwd, Wg_loop, b_fwd, b_bwd, b_loop, bg_fwd, bg_bwd, bg_loop):
        import jax, jax.numpy as jnp
        import numpy as np
        D_MODEL = 128
        NUM_REL = 40

        def _direction(x, W, Wg, b, bg, adj, rel_ids):
            h = x @ W.T
            g = h @ Wg.T
            vals = (h[:, :, None, :] + b) * jax.nn.sigmoid(g[:, :, None, :] + bg)
            onehot = (adj[..., None] == rel_ids).astype(h.dtype)
            return jnp.einsum('bnmr,bmrd->bnd', onehot, vals)
        rels = jnp.arange(2, NUM_REL + 1, dtype=adj_mat.dtype)
        rel1 = jnp.array([1], dtype=adj_mat.dtype)
        adj_t = jnp.swapaxes(adj_mat, -1, -2)
        out = _direction(node, W_fwd, Wg_fwd, b_fwd, bg_fwd, adj_mat, rels)
        out = out + _direction(node, W_bwd, Wg_bwd, b_bwd, bg_bwd, adj_t, rels)
        out = out + _direction(node, W_loop, Wg_loop, b_loop, bg_loop, adj_t, rel1)
        return jax.nn.relu(out)

    def _L1_gnn_ref(feature, graph, W_w, W_b, Q_w, Q_b, K_w, K_b):
        import jax, jax.numpy as jnp
        import numpy as np
        D = 128
        B, N = (16, 512)
        NEG_SLOPE = 0.2
        SCALE = float(np.sqrt(D))
        h = jnp.einsum('bnd,ed->bne', feature, W_w) + W_b
        q = jnp.einsum('bnd,ed->bne', h, Q_w) + Q_b
        k = jnp.einsum('bnd,ed->bne', h, K_w) + K_b
        e = jnp.einsum('bnd,bmd->bnm', q, k) / SCALE
        e = jnp.where(e >= 0, e, NEG_SLOPE * e)
        e = jnp.where(graph == 0, jnp.float32(-1000000000.0), e)
        a = jax.nn.softmax(e, axis=2)
        out = jax.nn.relu(jnp.einsum('bnm,bmd->bnd', a, h))
        return out
    h = jnp.maximum(_layernorm(x, axis=-1), 0.0)
    x = x + _L0_gnn_ref(h, nodemask, adj, L0_gnn_W_fwd, L0_gnn_W_bwd, L0_gnn_W_loop, L0_gnn_Wg_fwd, L0_gnn_Wg_bwd, L0_gnn_Wg_loop, L0_gnn_b_fwd, L0_gnn_b_bwd, L0_gnn_b_loop, L0_gnn_bg_fwd, L0_gnn_bg_bwd, L0_gnn_bg_loop)
    h = jnp.maximum(_layernorm(x, axis=-1), 0.0)
    x = x + _L1_gnn_ref(h, adj, L1_gnn_W_w, L1_gnn_W_b, L1_gnn_Q_w, L1_gnn_Q_b, L1_gnn_K_w, L1_gnn_K_b)
    return x

_drawn_inputs = setup_inputs


def setup_inputs(seed=0):
    import zlib

    import numpy as np

    out = dict(_drawn_inputs(seed))
    spreads = {}
    factors = {'L0_gnn_Wg_loop': 22.264,
     'L0_gnn_bg_loop': 27.859,
     'L1_gnn_Q_w': 8.0,
     'L1_gnn_Q_b': 8.0,
     'L1_gnn_K_w': 8.0,
     'L1_gnn_K_b': 55.626}
    for name, (base, spread) in spreads.items():
        noise = np.random.default_rng([zlib.crc32(name.encode()), seed]).standard_normal(out[name].shape)
        drawn = base * np.exp(spread * noise) if base else spread * noise
        out[name] = jnp.asarray(drawn.astype(out[name].dtype))
    for name, factor in factors.items():
        out[name] = (out[name] * factor).astype(out[name].dtype)
    return out
```

```python
from contextlib import ExitStack

import concourse.bass as bass
from concourse import mybir

F32 = mybir.dt.float32
BF16 = mybir.dt.bfloat16
I32 = mybir.dt.int32
ALU = mybir.AluOpType
ACT = mybir.ActivationFunctionType
AX = mybir.AxisListType

B, N, D = 64, 128, 128
PER = 4
GROUPS = B // PER
W = PER * D
RING = 4
RELS = 39
EPS = 1e-5
SLOPE = 0.2
SCALE = 1.0 / float(D) ** 0.5
MASKED = -(2.0 ** 100)
SPREAD = 32
PLAIN_SUM = 0.25 * W

FIRST, FULL, LAST = -2, 2, GROUPS + 1
CONSTANTS = 6
LOOPS = (GROUPS - 2 - FULL) // RING
AFTER = FULL + RING * LOOPS


NAMES = (
    "stats0 rstd0 xn0 h0_turned h0T hg tanh vals onehot agg x1 stats1 rstd1 xn1 h1_turned h1T v vT hw hwS "
    "masked scores logits p p_turned pT pv rinv att y counted bn var_eps steep extra"
).split()
DMA_NAMES = ("x_in", "adj_in", "y_out")
OPEN = {"p_turned": 1, "pv": 1, "scores": 1, "p": 1, "att": 1, "pT": 1, "rinv": 1, "logits": 1, "y": 1, "y_out": 16}


def semaphores(sem, tag):
    S = {name: sem(f"{tag}_{name}") for name in NAMES}
    return S | {name: [sem(f"{tag}_{name}{r}") for r in range(RING)] for name in DMA_NAMES}


def start_counts(engine, S, *names):
    for name in names:
        for sem in S[name] if name in DMA_NAMES else [S[name]]:
            engine.sem_inc(sem, OPEN[name])


def wait(engine, S, name, value, at=None):
    if isinstance(value, int) and value <= 0:
        return
    engine.wait_ge(S[name] if at is None else S[name][at], value + OPEN.get(name, 0))


def apart(engine, j, passed):
    if not isinstance(j, int):
        engine.sem_inc(passed, 1)


def lin(j, c, per=1, plus=0):
    if isinstance(j, int):
        return per * (4 * j + c) + plus
    k = per * c + plus
    return j * (4 * per) + k if k else j * (4 * per)


def dma_round(j, c):
    r = c // RING + 1
    if isinstance(j, int):
        return 16 * (j + r)
    return j * 16 + 16 * r


def has(j, c):
    return not isinstance(j, int) or 0 <= c < GROUPS


def slots(engine, run):
    for c in range(FIRST, FULL):
        run(0, c)
    with engine.Fori(0, LOOPS, 1) as j:
        for u in range(RING):
            run(j, FULL + u)
    for c in range(AFTER, LAST + 1):
        run(0, c)


def build(nc, t, out):
    x_dram = t["x"].rearrange("(g b) n d -> g n b d", b=PER)
    adj_dram = t["adj"].rearrange("(g b) n m -> g n b m", b=PER)
    out_dram = out.rearrange("(g b) n d -> g n b d", b=PER)

    with ExitStack() as ctx:
        def sb(name, shape, dt=F32):
            return ctx.enter_context(nc.sbuf_tensor(name, shape, dt))

        def bank(name, cols=512):
            return ctx.enter_context(nc.psum_tensor(name, [128, cols], F32))

        def sem(name):
            return ctx.enter_context(nc.semaphore(name))

        pool_of_tiles = sb("pool_of_tiles", [128, 20 * W])
        tiles = iter(range(20))

        def ring(count):
            return [pool_of_tiles[:, k * W:(k + 1) * W] for k in (next(tiles) for _ in range(count))]

        x = ring(RING)
        adj = [sb(f"adj{r}", [128, W], I32) for r in range(RING)]
        x1 = ring(RING)
        y = ring(RING)
        two = range(2)
        xn0 = ring(2)
        xn1 = ring(2)
        h0T = ring(2)
        h1T = ring(2)
        th = [sb(f"th{r}", [128, W]) for r in two]
        vals = [sb(f"vals{r}", [128, W]) for r in two]
        onehot = [sb(f"onehot{r}", [128, W]) for r in two]
        masked = [sb(f"masked{r}", [128, W], BF16) for r in two]
        vT = [sb(f"vT{r}", [128, W]) for r in two]
        hW = [sb(f"hW{r}", [128, PER, D + 1]) for r in two]
        steep = sb("steep", [128, W])
        logits = [sb(f"logits{r}", [128, W]) for r in two]
        neg_max = [sb(f"neg_max{r}", [128, PER]) for r in two]
        p = [sb(f"p{r}", [128, W]) for r in two]
        p_sum = [sb(f"p_sum{r}", [128, PER]) for r in two]
        rinv = [sb(f"rinv{r}", [128, PER]) for r in two]
        pT = [sb(f"pT{r}", [128, W]) for r in two]
        att = [sb(f"att{r}", [128, W]) for r in two]
        bn = sb("bn", [128, PER, 6])
        mv = [sb(f"mv{k}", [128, PER, 2]) for k in two]
        var_eps = [sb(f"var_eps{k}", [128, PER]) for k in two]
        rstd = [sb(f"rstd{k}", [128, PER]) for k in two]
        counted = sb("counted", [128, GROUPS])
        counted_out = sb("counted_out", [128, W], BF16)

        ident = sb("ident", [128, 128])
        masker = sb("masker", [128, 128], BF16)
        spread = sb("spread", [128, 128], BF16)
        minus_half = sb("minus_half", [128, PER])
        W_loop, Wg_loop, Q_w, K_w = (sb(n, [128, 128]) for n in ("W_loop", "Wg_loop", "Q_w", "K_w"))
        W_wb = sb("W_wb", [128, D + 1])
        qk_b = sb("qk_b", [128, 2])
        WgT, QwT, KwT = (sb(n, [128, 128]) for n in ("WgT", "QwT", "KwT"))
        A = sb("A", [128, 128])
        C = sb("C", [128, 128])
        a_col = sb("a_col", [128, 1])
        c_col = sb("c_col", [128, 1])
        w_hg = sb("w_hg", [128, 2 * D])
        w_hw = sb("w_hw", [128, D + 1])
        w_v = sb("w_v", [128, 128])
        v_bias = sb("v_bias", [128, 1])
        rows = sb("rows", [128, 3 * D + 1])
        rest = sb("rest", [128, 3 * D + 1])
        high = sb("high", [128, 3 * D + 1], BF16)
        middle = sb("middle", [128, 3 * D + 1], BF16)
        parts = sb("parts", [128, 3 * D + 1], BF16)
        over = sb("over", [128, GROUPS])
        over_row = sb("over_row", [128, 1])
        flag = sb("flag", [1, 1], I32)

        rel_b = pool_of_tiles[:, 0:RELS * 2 * D].rearrange("p (r k) -> p r k", r=RELS)
        rel_bg = sb("rel_bg", [128, RELS, 2 * D])
        rel_w = sb("rel_w", [128, 4 * D])
        rel_natural = sb("rel_natural", [128, 4 * D])
        rel_WgT = sb("rel_WgT", [128, 2 * D])
        extra = sb("extra", [128, B * D])
        gx = sb("gx", [128, D])
        gadj = sb("gadj", [128, D], I32)
        gbn = sb("gbn", [128, 6])
        gmv = sb("gmv", [128, 2])
        gvar = sb("gvar", [128, 1])
        grstd = sb("grstd", [128, 1])
        gxn = sb("gxn", [128, D])
        ghT = sb("ghT", [128, D])
        adj_both = sb("adj_both", [128, 2 * D])
        ghg = sb("ghg", [128, 4 * D])
        relation = sb("relation", [128, 1])
        gate_in = sb("gate_in", [128, 2 * D])
        gate = sb("gate", [128, 2 * D])
        lifted = sb("lifted", [128, 2 * D])
        gvals = sb("gvals", [128, 2 * D])
        half_hot = sb("half_hot", [128, 2 * D])
        zeros = sb("zeros", [128, D], BF16)
        constants = sem("constants")
        passed = sem("passed")

        b_hg = bank("b_hg", 1024)
        b_e = bank("b_e")
        b_pT = bank("b_pT")
        b_h1 = bank("b_h1")
        b_v = bank("b_v")
        b_agg = bank("b_agg")
        b_pv = bank("b_pv")
        hg_view = b_hg[:, :].rearrange("p (b k) -> p b k", b=PER)

        def graph(tile, b):
            return tile[:, b * D:(b + 1) * D]

        def twice(row):
            return row.unsqueeze(1).to_broadcast([128, 2, row.shape[1]])

        def by_graph(tile):
            return tile[:, :].rearrange("p (b k) -> p b k", b=PER)


        def sync_loads(sp, S, j, c):
            r = c % RING
            wait(sp, S, "x1", lin(j, c, plus=-RING + 1))
            sp.dma_start(x[r][:, :].rearrange("p (b d) -> p b d", b=PER), x_dram[lin(j, c)]).then_inc(S["x_in"][r], 16)
            wait(sp, S, "masked", lin(j, c, plus=-RING + 1))
            wait(sp, S, "counted", lin(j, c, plus=-RING + 1))
            sp.dma_start(adj[r][:, :].rearrange("p (b d) -> p b d", b=PER), adj_dram[lin(j, c)])\
              .then_inc(S["adj_in"][r], 16)

        def sync_store(sp, S, j, c):
            r = c % RING
            wait(sp, S, "y", lin(j, c, plus=1))
            sp.dma_start(out_dram[lin(j, c)], y[r][:, :].rearrange("p (b d) -> p b d", b=PER)).then_inc(S["y_out"][r], 16)

        def sync_program(sp, S):
            start_counts(sp, S, "y_out")
            behind = RING + 3
            for g in range(2 * RING):
                sync_loads(sp, S, 0, g)
                if g >= behind:
                    sync_store(sp, S, 0, g - behind)
            with sp.Fori(2, GROUPS // RING, 1) as j:
                for u in range(RING):
                    sync_loads(sp, S, j, u)
                    sync_store(sp, S, j, u - behind)
            for g in range(GROUPS - behind, GROUPS):
                sync_store(sp, S, 0, g)
            for r in range(RING):
                wait(sp, S, "y_out", 16 * GROUPS // RING, r)

        def pool_slot(pool, S, j, c):
            g = c + 1
            if has(j, g):
                r = g % 2
                pool.wait_ge(S["adj_in"][g % RING], dma_round(j, g))
                wait(pool, S, "agg", lin(j, g, plus=-1))
                apart(pool, j, passed)
                pool.tensor_scalar(onehot[r][:, :], adj[g % RING][:, :], 1.0, None, ALU.is_equal)\
                    .then_inc(S["onehot"], 1)
            g = c
            if has(j, g):
                r = g % 2
                wait(pool, S, "scores", lin(j, g, plus=-1))
                apart(pool, j, passed)
                pool.tensor_scalar(masked[r][:, :], adj[g % RING][:, :], 0.0, None, ALU.is_equal)\
                    .then_inc(S["masked"], 1)
            for k, g, stats, done in ((0, c + 2, S["stats0"], S["rstd0"]), (1, c, S["stats1"], S["rstd1"])):
                if has(j, g):
                    pool.wait_ge(stats, lin(j, g, plus=1))
                    apart(pool, j, passed)
                    pool.tensor_scalar(var_eps[k][:, :], mv[k][:, :, 1], EPS, None, ALU.add).then_inc(S["var_eps"], 1)
                    pool.wait_ge(S["var_eps"], var_eps_count(j, c, k))
                    pool.tensor_tensor(rstd[k][:, :], var_eps[k][:, :], minus_half[:, :], ALU.pow).then_inc(done, 1)
            g = c - 2
            if has(j, g):
                r = g % RING
                wait(pool, S, "att", lin(j, g, plus=1))
                wait(pool, S, "y_out", dma_round(j, g - RING), r)
                pool.tensor_tensor(y[r][:, :], att[g % 2][:, :], x1[r][:, :], ALU.add).then_inc(S["y"], 1)

        def pool_program(pool, S):
            start_counts(pool, S, "y")
            slots(pool, lambda j, c: pool_slot(pool, S, j, c))

        def var_eps_count(j, c, k):
            if not isinstance(j, int):
                return lin(j, c, 2, 3 + k)
            first, second = min(c + 3, GROUPS), c if k == 0 else c + 1
            return first + max(second, 0)

        def scalar_slot(act, S, j, c):
            g = c - 2
            if has(j, g):
                r = g % 2
                wait(act, S, "p_turned", lin(j, g))
                wait(act, S, "rinv", lin(j, g))
                for b in range(PER):
                    wait(act, S, "logits", lin(j, g, PER, b + 1))
                    ins = nc.scalar.activation(graph(p[r], b), graph(logits[r], b), ACT.Exp,
                                               bias=neg_max[r][:, b:b + 1], scale=-1.0, accum_out=p_sum[r][:, b:b + 1])
                ins.then_inc(S["p"], 1)
            g = c
            if has(j, g):
                r = g % 2
                act.wait_ge(S["hg"], lin(j, g, plus=1))
                wait(act, S, "vals", lin(j, g, plus=-1))
                nc.scalar.activation(by_graph(th[r]), hg_view[:, :, D:2 * D], ACT.Tanh, scale=0.5).then_inc(S["tanh"], 1)
            g = c - 2
            if has(j, g):
                r = g % 2
                wait(act, S, "p_turned", lin(j, g, plus=1))
                wait(act, S, "pv", lin(j, g))
                nc.scalar.activation(pT[r][:, :], b_pT[:, :], ACT.Copy).then_inc(S["pT"], 1)
            g = c + 1
            if has(j, g):
                r = g % 2
                act.wait_ge(S["h0_turned"], lin(j, g, plus=1))
                wait(act, S, "hg", lin(j, g, plus=-1))
                nc.scalar.activation(h0T[r][:, :], b_v[:, :], ACT.Relu).then_inc(S["h0T"], 1)
            g = c - 1
            if has(j, g):
                r = g % 2
                act.wait_ge(S["h1_turned"], lin(j, g, plus=1))
                wait(act, S, "scores", lin(j, g, plus=-1))
                nc.scalar.activation(h1T[r][:, :], b_h1[:, :], ACT.Relu).then_inc(S["h1T"], 1)
            g = c - 1
            if has(j, g):
                r = g % 2
                act.wait_ge(S["v"], lin(j, g, plus=1))
                wait(act, S, "scores", lin(j, g, plus=-1))
                nc.scalar.activation(vT[r][:, :], b_v[:, :], ACT.Identity, bias=v_bias[:, 0:1]).then_inc(S["vT"], 1)
                act.wait_ge(S["hw"], lin(j, g, plus=1))
                wait(act, S, "pv", lin(j, g, plus=-1))
                wait(act, S, "logits", lin(j, g, PER, -PER))
                nc.scalar.activation(hW[r][:, :, :], hg_view[:, :, 0:D + 1], ACT.Copy).then_inc(S["hwS"], 1)
            g = c - 2
            if has(j, g):
                r = g % 2
                wait(act, S, "pv", lin(j, g, plus=1))
                wait(act, S, "rinv", lin(j, g, plus=1))
                wait(act, S, "y", lin(j, g))
                for b in range(PER):
                    ins = nc.scalar.activation(graph(att[r], b), graph(b_pv, b), ACT.Relu, scale=rinv[r][:, b:b + 1])
                ins.then_inc(S["att"], 1)
            g = c + 1
            if has(j, g):
                act.wait_ge(S["adj_in"][g % RING], dma_round(j, g))
                wait(act, S, "counted", lin(j, g))
                col = lin(j, g)
                at = counted[:, col:col + 1] if isinstance(col, int) else counted[:, bass.ds(col, 1)]
                nc.scalar.activation(counted_out[:, :], adj[g % RING][:, :], ACT.Square, bias=minus_half[:, 0:1],
                                     accum_out=at).then_inc(S["counted"], 1)

        def norm_stats(dve, S, j, tile, k, done, bn_count):
            for b in range(PER):
                ins = nc.vector.bn_stats(bn[:, b, :], graph(tile, b))
            ins.then_inc(S["bn"], 1)
            dve.wait_ge(S["bn"], bn_count)
            apart(dve, j, passed)
            for b in range(PER):
                ins = nc.vector.bn_aggr(mv[k][:, b, :], bn[:, b, :])
            ins.then_inc(done, 1)

        def norm_apply(tile_out, tile, k):
            for b in range(PER):
                ins = nc.vector.tensor_scalar(graph(tile_out, b), graph(tile, b), mv[k][:, b, 0:1],
                                              rstd[k][:, b:b + 1], ALU.subtract, ALU.mult)
            return ins

        def bn_count(j, c, k):
            return var_eps_count(j, c, k)

        def vector_slot(dve, S, j, c, extra=None):
            g = c - 2
            if has(j, g):
                r = g % 2
                wait(dve, S, "p", lin(j, g))
                dve.wait_ge(S["hwS"], lin(j, g, plus=1))
                wait(dve, S, "scores", lin(j, g, plus=1))
                for b in range(PER + 1):
                    if b < PER:
                        
                        nc.vector.tensor_scalar(graph(steep, b), graph(b_e, b), SLOPE - 1.0, hW[r][:, b, D:D + 1],
                                                ALU.mult, ALU.max).then_inc(S["steep"], 1)
                    if b >= 1:
                        dve.wait_ge(S["steep"], lin(j, g, PER, b))
                        apart(dve, j, passed)
                        nc.vector.tensor_tensor_reduce(graph(logits[r], b - 1), graph(b_e, b - 1), graph(steep, b - 1),
                                                       -1.0, 3.0e38, ALU.add, ALU.min,
                                                       neg_max[r][:, b - 1:b]).then_inc(S["logits"], 1)
            g = c - 1
            if has(j, g):
                dve.wait_ge(S["rstd1"], lin(j, g, plus=1))
                wait(dve, S, "h1_turned", lin(j, g, plus=-1))
                norm_apply(xn1[g % 2], x1[g % RING], 1).then_inc(S["xn1"], 1)
            g = c
            if has(j, g):
                r = g % 2
                dve.wait_ge(S["tanh"], lin(j, g, plus=1))
                wait(dve, S, "agg", lin(j, g, plus=-1))
                nc.vector.scalar_tensor_tensor(by_graph(vals[r]), by_graph(th[r]), 1.0, hg_view[:, :, 0:D],
                                               ALU.add, ALU.mult).then_inc(S["vals"], 1)
            g = c + 2
            if has(j, g):
                dve.wait_ge(S["x_in"][g % RING], dma_round(j, g))
                norm_stats(dve, S, j, x[g % RING], 0, S["stats0"], bn_count(j, c, 0))
            g = c - 2
            if has(j, g):
                r = g % 2
                wait(dve, S, "p", lin(j, g, plus=1))
                wait(dve, S, "att", lin(j, g))
                nc.vector.reciprocal(rinv[r][:, :], p_sum[r][:, :]).then_inc(S["rinv"], 1)
            g = c
            if has(j, g):
                r = g % RING
                dve.wait_ge(S["agg"], lin(j, g, plus=1))
                wait(dve, S, "y", lin(j, g, plus=-RING + 2))
                if extra is None:
                    nc.vector.scalar_tensor_tensor(x1[r][:, :], b_agg[:, :], 0.0, x[r][:, :], ALU.max, ALU.add)\
                        .then_inc(S["x1"], 1)
                else:
                    at = lin(j, g, W)
                    more = extra[:, at:at + W] if isinstance(at, int) else extra[:, bass.ds(at, W)]
                    nc.vector.tensor_tensor(steep[:, :], b_agg[:, :], more, ALU.add).then_inc(S["extra"], 1)
                    dve.wait_ge(S["extra"], lin(j, g, plus=1))
                    nc.vector.scalar_tensor_tensor(x1[r][:, :], steep[:, :], 0.0, x[r][:, :], ALU.max, ALU.add)\
                        .then_inc(S["x1"], 1)
                dve.wait_ge(S["x1"], lin(j, g, plus=1))
                norm_stats(dve, S, j, x1[r], 1, S["stats1"], bn_count(j, c, 1))
            g = c + 2
            if has(j, g):
                dve.wait_ge(S["rstd0"], lin(j, g, plus=1))
                wait(dve, S, "h0_turned", lin(j, g, plus=-1))
                norm_apply(xn0[g % 2], x[g % RING], 0).then_inc(S["xn0"], 1)

        def tensor_slot(pe, S, j, c):
            def turn(bank_, tile):
                for b in range(PER):
                    ins = nc.tensor.transpose(graph(bank_, b), graph(tile, b), ident[:, :])
                return ins

            g = c
            if has(j, g):
                r = g % 2
                pe.wait_ge(S["h0T"], lin(j, g, plus=1))
                wait(pe, S, "hwS", lin(j, g, plus=-1))
                for b in range(PER):
                    if b % 2 == 0:
                        nc.tensor.matmul(hg_view[:, b:b + 2, :], spread[:, :], twice(parts[:, 0:2 * D]),
                                         start=True, stop=False)
                    ins = nc.tensor.matmul(hg_view[:, b, :], graph(h0T[r], b), w_hg[:, :], start=False, stop=b % 2 == 1)
                ins.then_inc(S["hg"], 1)
            g = c + 1
            if has(j, g):
                pe.wait_ge(S["xn0"], lin(j, g, plus=1))
                wait(pe, S, "vT", lin(j, g, plus=-2))
                turn(b_v, xn0[g % 2]).then_inc(S["h0_turned"], 1)
            g = c - 2
            if has(j, g):
                wait(pe, S, "p", lin(j, g, plus=1))
                wait(pe, S, "pT", lin(j, g))
                turn(b_pT, p[g % 2]).then_inc(S["p_turned"], 1)
            g = c - 1
            if has(j, g):
                pe.wait_ge(S["xn1"], lin(j, g, plus=1))
                wait(pe, S, "h1T", lin(j, g))
                turn(b_h1, xn1[g % 2]).then_inc(S["h1_turned"], 1)
            g = c - 2
            if has(j, g):
                r = g % 2
                wait(pe, S, "pT", lin(j, g, plus=1))
                wait(pe, S, "att", lin(j, g))
                for b in range(PER):
                    ins = nc.tensor.matmul(graph(b_pv, b), graph(pT[r], b), hW[r][:, b, 0:D], start=True, stop=True)
                ins.then_inc(S["pv"], 1)
            g = c
            if has(j, g):
                r = g % 2
                pe.wait_ge(S["vals"], lin(j, g, plus=1))
                pe.wait_ge(S["onehot"], lin(j, g, plus=1))
                wait(pe, S, "x1", lin(j, g))
                for b in range(PER):
                    ins = nc.tensor.matmul(graph(b_agg, b), graph(onehot[r], b), graph(vals[r], b), start=True, stop=True)
                ins.then_inc(S["agg"], 1)
            g = c - 1
            if has(j, g):
                r = g % 2
                pe.wait_ge(S["h1T"], lin(j, g, plus=1))
                after = lambda k: lin(j, g, plus=k) if not isinstance(j, int) else min(g + k, GROUPS)
                pe.wait_ge(S["h0T"], after(3))
                nc.tensor.matmul(b_v[:, :], w_v[:, :], h1T[r][:, :], start=True, stop=True).then_inc(S["v"], 1)
                pe.wait_ge(S["vals"], after(2))
                for b in range(PER):
                    if b % 2 == 0:
                        nc.tensor.matmul(hg_view[:, b:b + 2, 0:D + 1], spread[:, :], twice(parts[:, 2 * D:3 * D + 1]),
                                         start=True, stop=False)
                    ins = nc.tensor.matmul(hg_view[:, b, 0:D + 1], graph(h1T[r], b), w_hw[:, :], start=False,
                                           stop=b % 2 == 1)
                ins.then_inc(S["hw"], 1)
                pe.wait_ge(S["masked"], lin(j, g, plus=1))
                wait(pe, S, "logits", lin(j, g, PER))
                pe.wait_ge(S["vT"], lin(j, g, plus=1))
                nc.tensor.matmul(b_e[:, :], masker[:, :], masked[r][:, :], start=True, stop=False)
                for b in range(PER):
                    ins = nc.tensor.matmul(graph(b_e, b), graph(vT[r], b), graph(h1T[r], b), start=False,
                                           stop=b == PER - 1)
                ins.then_inc(S["scores"], 1)


        main = semaphores(sem, "m")
        weights_in = sem("weights_in")
        rows_in = sem("rows_in")
        scores_in = sem("scores_in")
        turned = sem("turned")
        folded = sem("folded")
        flagged = sem("flagged")
        flag_turned = sem("flag_turned")

        block = nc.Block()
        with block:
            @block.sync
            def _(sp):
                sync_program(sp, main)

            @block.gpsimd
            def _(pool):
                pool.memset(ident[:, :], 0.0).then_inc(constants, 1)
                pool.memset(masker[:, :], 0.0).then_inc(constants, 1)
                pool.memset(spread[:, :], 1.0 / SPREAD).then_inc(constants, 1)
                pool.memset(minus_half[:, :], -0.5).then_inc(constants, 1)
                pool.wait_ge(constants, 2)
                for m, fill in ((ident, 1.0), (masker, MASKED)):
                    pool.affine_select(out=m[:, :], in_=m[:, :], compare_op=ALU.not_equal, fill=fill, base=0,
                                       pattern=[[-1, 128]], channel_multiplier=1).then_inc(constants, 1)
                pool.wait_ge(constants, CONSTANTS)
                pool_program(pool, main)

            @block.scalar
            def _(act):
                for name, tile in (("L0_gnn_W_loop", W_loop), ("L0_gnn_Wg_loop", Wg_loop)):
                    act.dma_start(tile[:, :], t[name]).then_inc(weights_in, 16)
                act.dma_start(rows[:, 0:D], t["L0_gnn_b_loop"].to_broadcast([128, D])).then_inc(rows_in, 16)
                act.dma_start(rows[:, D:2 * D], t["L0_gnn_bg_loop"].to_broadcast([128, D])).then_inc(rows_in, 16)
                act.dma_start(rows[:, 2 * D:3 * D], t["L1_gnn_W_b"].unsqueeze(0).to_broadcast([128, D]))\
                   .then_inc(rows_in, 16)
                act.dma_start(W_wb[:, 0:D], t["L1_gnn_W_w"]).then_inc(scores_in, 16)
                act.dma_start(Q_w[:, :], t["L1_gnn_Q_w"]).then_inc(scores_in, 16)
                act.dma_start(K_w[:, :], t["L1_gnn_K_w"]).then_inc(scores_in, 16)
                act.dma_start(W_wb[:, D:D + 1], t["L1_gnn_W_b"].unsqueeze(1)).then_inc(scores_in, 16)
                act.dma_start(qk_b[:, 0:1], t["L1_gnn_Q_b"].unsqueeze(1)).then_inc(scores_in, 16)
                act.dma_start(qk_b[:, 1:2], t["L1_gnn_K_b"].unsqueeze(1)).then_inc(scores_in, 16)
                act.wait_ge(constants, CONSTANTS)
                start_counts(act, main, "p", "att", "pT")

                def run(j, c):
                    if isinstance(j, int) and c == 0:
                        act.wait_ge(folded, 12)
                    scalar_slot(act, main, j, c)
                slots(act, run)

            @block.vector
            def _(dve):
                def split_rows(lo, hi, count):
                    s = slice(lo, hi)
                    nc.vector.tensor_copy(high[:, s], rows[:, s]).then_inc(folded, 1)
                    dve.wait_ge(folded, count + 1)
                    nc.vector.tensor_tensor(rest[:, s], rows[:, s], high[:, s], ALU.subtract).then_inc(folded, 1)
                    dve.wait_ge(folded, count + 2)
                    nc.vector.tensor_copy(middle[:, s], rest[:, s]).then_inc(folded, 1)
                    dve.wait_ge(folded, count + 3)
                    nc.vector.memset(parts[96:128, s], 0.0)
                    nc.vector.tensor_copy(parts[0:32, s], high[0:32, s])
                    nc.vector.tensor_copy(parts[32:64, s], middle[32:64, s])
                    nc.vector.tensor_tensor(parts[64:96, s], rest[64:96, s], middle[64:96, s], ALU.subtract)\
                        .then_inc(folded, 1)

                def setup_relational():
                    dve.wait_ge(rows_in, 48)
                    nc.vector.tensor_scalar(rows[:, 0:D], rows[:, 0:D], 0.5, None, ALU.mult).then_inc(folded, 1)
                    dve.wait_ge(folded, 1)
                    split_rows(0, 2 * D, 1)
                    dve.wait_ge(turned, 1)
                    nc.vector.tensor_copy(WgT[:, :], b_e[:, D:2 * D]).then_inc(folded, 1)
                    nc.vector.tensor_scalar(w_hg[:, 0:D], b_e[:, 0:D], 0.5, None, ALU.mult)
                    dve.wait_ge(turned, 3)
                    nc.vector.tensor_copy(w_hg[:, D:2 * D], b_agg[:, 0:D]).then_inc(folded, 1)

                def setup_attention():
                    dve.wait_ge(turned, 2)
                    nc.vector.tensor_copy(w_hw[:, 0:D], b_pv[:, 0:D])
                    nc.vector.tensor_copy(QwT[:, :], b_pv[:, D:2 * D])
                    nc.vector.tensor_copy(KwT[:, :], b_pv[:, 2 * D:3 * D]).then_inc(folded, 1)
                    dve.wait_ge(turned, 4)
                    nc.vector.tensor_copy(A[:, :], b_pv[:, 0:D])
                    nc.vector.tensor_copy(C[:, :], b_pv[:, 2 * D:3 * D])
                    nc.vector.tensor_tensor(a_col[:, :], b_pv[:, D:D + 1], qk_b[:, 0:1], ALU.add)
                    nc.vector.tensor_tensor(c_col[:, :], b_pv[:, 3 * D:3 * D + 1], qk_b[:, 1:2], ALU.add)\
                        .then_inc(folded, 1)
                    dve.wait_ge(turned, 5)
                    nc.vector.tensor_scalar(w_v[:, :], b_pv[:, 0:D], SCALE, None, ALU.mult)
                    nc.vector.tensor_scalar(w_hw[:, D:D + 1], b_pv[:, D + 1:D + 2], SCALE * (1.0 - SLOPE), None, ALU.mult)
                    nc.vector.tensor_scalar(rows[:, 3 * D:3 * D + 1], b_pv[:, D + 2:D + 3], SCALE * (1.0 - SLOPE), None,
                                            ALU.mult).then_inc(folded, 1)
                    nc.vector.tensor_scalar(v_bias[:, :], b_pv[:, D:D + 1], SCALE, None, ALU.mult).then_inc(folded, 1)
                    dve.wait_ge(folded, 11)
                    nc.vector.memset(rest[:, 0:1], 0.0).then_inc(folded, 1)
                    dve.wait_ge(folded, 12)
                    split_rows(2 * D, 3 * D + 1, 12)

                start_counts(dve, main, "rinv", "logits")

                def run(j, c):
                    vector_slot(dve, main, j, c)
                    if isinstance(j, int) and c == FIRST:
                        setup_relational()
                    if isinstance(j, int) and c == FIRST + 1:
                        setup_attention()
                    if isinstance(j, int) and c == GROUPS:
                        dve.wait_ge(main["counted"], GROUPS)
                        nc.vector.tensor_scalar(over[:, :], counted[:, :], PLAIN_SUM + 1.0, None, ALU.is_gt)\
                            .then_inc(flagged, 1)
                        dve.wait_ge(flagged, 1)
                        nc.vector.tensor_reduce(over_row[:, :], over[:, :], AX.X, ALU.max).then_inc(flagged, 1)
                slots(dve, run)
                dve.wait_ge(flag_turned, 1)
                nc.vector.tensor_reduce(flag[:, :], b_agg[0:1, 0:128], AX.X, ALU.max).then_inc(flagged, 1)

            @block.tensor
            def _(pe):
                start_counts(pe, main, "p_turned", "pv", "scores")
                pe.wait_ge(constants, CONSTANTS)
                pe.wait_ge(weights_in, 32)
                nc.tensor.transpose(b_e[:, 0:D], W_loop[:, :], ident[:, :])
                nc.tensor.transpose(b_e[:, D:2 * D], Wg_loop[:, :], ident[:, :]).then_inc(turned, 1)
                pe.wait_ge(scores_in, 96)
                nc.tensor.transpose(b_pv[:, 0:D], W_wb[:, 0:D], ident[:, :])
                nc.tensor.transpose(b_pv[:, D:2 * D], Q_w[:, :], ident[:, :])
                nc.tensor.transpose(b_pv[:, 2 * D:3 * D], K_w[:, :], ident[:, :]).then_inc(turned, 1)
                pe.wait_ge(folded, 6)
                nc.tensor.matmul(b_agg[:, 0:D], W_loop[:, :], WgT[:, :], start=True, stop=True).then_inc(turned, 1)
                tensor_slot(pe, main, 0, FIRST)
                tensor_slot(pe, main, 0, FIRST + 1)
                pe.wait_ge(folded, 8)
                nc.tensor.matmul(b_pv[:, 0:D + 1], QwT[:, :], W_wb[:, :], start=True, stop=True)
                nc.tensor.matmul(b_pv[:, 2 * D:3 * D + 1], KwT[:, :], W_wb[:, :], start=True, stop=True)\
                  .then_inc(turned, 1)
                pe.wait_ge(folded, 9)
                nc.tensor.matmul(b_pv[:, 0:D], A[:, :], C[:, :], start=True, stop=True)
                nc.tensor.matmul(b_pv[:, D:D + 1], C[:, :], a_col[:, :], start=True, stop=True)
                nc.tensor.matmul(b_pv[:, D + 1:D + 2], A[:, :], c_col[:, :], start=True, stop=True)
                nc.tensor.matmul(b_pv[:, D + 2:D + 3], a_col[:, 0:1].to_broadcast([128, 128]), c_col[:, :],
                                 start=True, stop=True).then_inc(turned, 1)
                pe.wait_ge(folded, 16)
                def run(j, c):
                    if isinstance(j, int) and c < 0:
                        return
                    tensor_slot(pe, main, j, c)
                slots(pe, run)
                pe.wait_ge(flagged, 2)
                pe.wait_ge(main["x1"], GROUPS)
                nc.tensor.transpose(b_agg[0:1, 0:128], over_row[:, :], ident[:, :]).then_inc(flag_turned, 1)


        again = semaphores(sem, "a")
        rel_in = sem("rel_in")
        rel_turned = sem("rel_turned")
        rel_folded = sem("rel_folded")
        gx_in = sem("gx_in")
        gadj_in = sem("gadj_in")
        g_bn = sem("g_bn")
        g_stats = sem("g_stats")
        g_var = sem("g_var")
        g_rstd = sem("g_rstd")
        g_xn = sem("g_xn")
        g_turned = sem("g_turned")
        g_hT = sem("g_hT")
        g_hg = sem("g_hg")
        g_ready = sem("g_ready")
        r_gate_in = sem("r_gate_in")
        r_gate = sem("r_gate")
        r_hot = sem("r_hot")
        r_vals = sem("r_vals")
        r_next = sem("r_next")
        r_summed = sem("r_summed")
        g_sum = sem("g_sum")
        g_extra = sem("g_extra")

        def on_flag(engine, program):
            with engine.If(engine.value_load(flag[0:1, 0:1]) > 0):
                program(engine)
                engine.sem_inc(passed, 1)

        def relation_loads(sp, i):
            sp.dma_start(gx[:, :], t["x"][i]).then_inc(gx_in, 16)
            sp.dma_start(gadj[:, :], t["adj"][i]).then_inc(gadj_in, 16)

        def sync_again(sp):
            for k, name in enumerate(("L0_gnn_W_fwd", "L0_gnn_W_bwd", "L0_gnn_Wg_fwd", "L0_gnn_Wg_bwd")):
                sp.dma_start(rel_natural[:, k * D:(k + 1) * D], t[name]).then_inc(rel_in, 16)
            for k, way in enumerate(("fwd", "bwd")):
                for tile, name in ((rel_b, "b"), (rel_bg, "bg")):
                    row = t[f"L0_gnn_{name}_{way}"].unsqueeze(0).to_broadcast([128, RELS, D])
                    sp.dma_start(tile[:, :, k * D:(k + 1) * D], row).then_inc(rel_in, 16)
            relation_loads(sp, 0)
            with sp.Fori(1, B, 1) as i:
                sp.wait_ge(g_xn, i)
                relation_loads(sp, i)
            sp.wait_ge(g_extra, B)
            sync_program(sp, again)

        def pool_again(pool):
            with pool.Fori(0, B, 1) as i:
                pool.wait_ge(g_stats, i + 1)
                pool.sem_inc(passed, 1)
                pool.tensor_scalar(gvar[:, :], gmv[:, 1:2], EPS, None, ALU.add).then_inc(g_var, 1)
                pool.wait_ge(g_var, i + 1)
                pool.tensor_tensor(grstd[:, :], gvar[:, :], minus_half[:, 0:1], ALU.pow).then_inc(g_rstd, 1)
            pool_program(pool, again)

        def scalar_again(act):
            with act.Fori(0, B, 1) as i:
                with act.Fori(0, RELS, 1) as r:
                    act.wait_ge(r_gate_in, i * RELS + r + 1)
                    nc.scalar.activation(gate[:, :], gate_in[:, :], ACT.Tanh, scale=0.5).then_inc(r_gate, 1)
            start_counts(act, again, "p", "att", "pT")
            slots(act, lambda j, c: scalar_slot(act, again, j, c))

        def vector_again(dve):
            nc.vector.memset(zeros[:, :], 0.0).then_inc(rel_folded, 1)
            dve.wait_ge(rel_turned, 1)
            nc.vector.tensor_copy(rel_WgT[:, :], b_e[:, 2 * D:4 * D]).then_inc(rel_folded, 1)
            nc.vector.tensor_copy(rel_w[:, 0:2 * D], b_e[:, 0:2 * D]).then_inc(rel_folded, 1)
            dve.wait_ge(rel_turned, 2)
            nc.vector.tensor_copy(rel_w[:, 2 * D:4 * D], b_pv[:, 0:2 * D]).then_inc(rel_folded, 1)
            dve.wait_ge(rel_in, 16 * 8)
            with dve.Fori(0, B, 1) as i:
                dve.wait_ge(gx_in, i * 16 + 16)
                nc.vector.bn_stats(gbn[:, :], gx[:, :]).then_inc(g_bn, 1)
                dve.wait_ge(g_bn, i + 1)
                dve.sem_inc(passed, 1)
                nc.vector.bn_aggr(gmv[:, :], gbn[:, :]).then_inc(g_stats, 1)
                dve.wait_ge(gadj_in, i * 16 + 16)
                nc.vector.tensor_copy(adj_both[:, D:2 * D], gadj[:, :])
                dve.wait_ge(g_rstd, i + 1)
                nc.vector.tensor_scalar(gxn[:, :], gx[:, :], gmv[:, 0:1], grstd[:, 0:1], ALU.subtract, ALU.mult)\
                    .then_inc(g_xn, 1)
                dve.wait_ge(g_turned, i + 1)
                nc.vector.tensor_scalar(ghT[:, :], b_h1[:, 0:D], 0.0, None, ALU.max)
                nc.vector.tensor_copy(adj_both[:, 0:D], b_h1[:, D:2 * D]).then_inc(g_hT, 1)
                dve.wait_ge(g_hg, i + 1)
                nc.vector.memset(relation[:, :], 2.0)
                nc.vector.tensor_copy(ghg[:, :], b_hg[:, 0:4 * D]).then_inc(g_ready, 1)
                dve.wait_ge(g_ready, i + 1)
                dve.sem_inc(passed, 1)
                with dve.Fori(0, RELS, 1) as r:
                    done = i * RELS + r
                    nc.vector.tensor_tensor(gate_in[:, :], ghg[:, 2 * D:4 * D], rel_bg[:, bass.ds(r, 1), :], ALU.add)\
                        .then_inc(r_gate_in, 1)
                    dve.wait_ge(r_summed, done + 1)
                    nc.vector.tensor_tensor(lifted[:, :], ghg[:, 0:2 * D], rel_b[:, bass.ds(r, 1), :], ALU.add)
                    nc.vector.tensor_scalar(half_hot[:, :], adj_both[:, :], relation[:, 0:1], 0.5, ALU.is_equal,
                                            ALU.mult).then_inc(r_hot, 1)
                    dve.wait_ge(r_hot, done + 1)
                    nc.vector.tensor_scalar(relation[:, :], relation[:, :], 1.0, None, ALU.add).then_inc(r_next, 1)
                    dve.wait_ge(r_gate, done + 1)
                    nc.vector.scalar_tensor_tensor(gvals[:, :], gate[:, :], 1.0, lifted[:, :], ALU.add, ALU.mult)\
                        .then_inc(r_vals, 1)
                    dve.wait_ge(r_next, done + 1)
                dve.wait_ge(g_sum, i + 1)
                nc.vector.tensor_copy(extra[:, bass.ds(i * D, D)], b_agg[:, 0:D]).then_inc(g_extra, 1)
            dve.wait_ge(g_extra, B)
            start_counts(dve, again, "rinv", "logits")
            slots(dve, lambda j, c: vector_slot(dve, again, j, c, extra))

        def tensor_again(pe):
            pe.sem_inc(r_summed, 1)
            pe.wait_ge(rel_in, 16 * 8)
            for k in range(4):
                ins = nc.tensor.transpose(b_e[:, k * D:(k + 1) * D], rel_natural[:, k * D:(k + 1) * D], ident[:, :])
            ins.then_inc(rel_turned, 1)
            pe.wait_ge(rel_folded, 2)
            for k in range(2):
                ins = nc.tensor.matmul(b_pv[:, k * D:(k + 1) * D], rel_natural[:, k * D:(k + 1) * D],
                                       rel_WgT[:, k * D:(k + 1) * D], start=True, stop=True)
            ins.then_inc(rel_turned, 1)
            pe.wait_ge(rel_folded, 4)
            with pe.Fori(0, B, 1) as i:
                pe.wait_ge(g_xn, i + 1)
                nc.tensor.transpose(b_h1[:, 0:D], gxn[:, :], ident[:, :])
                nc.tensor.transpose(b_h1[:, D:2 * D], adj_both[:, D:2 * D], ident[:, :]).then_inc(g_turned, 1)
                pe.wait_ge(g_hT, i + 1)
                nc.tensor.matmul(b_hg[:, 0:4 * D], ghT[:, :], rel_w[:, :], start=True, stop=True).then_inc(g_hg, 1)
                nc.tensor.matmul(b_agg[:, 0:D], zeros[:, :], zeros[:, :], start=True, stop=False)
                with pe.Fori(0, RELS, 1) as r:
                    pe.wait_ge(r_vals, i * RELS + r + 1)
                    for k in range(2):
                        ins = nc.tensor.matmul(b_agg[:, 0:D], half_hot[:, k * D:(k + 1) * D],
                                               gvals[:, k * D:(k + 1) * D], start=False, stop=False)
                    ins.then_inc(r_summed, 1)
                nc.tensor.matmul(b_agg[:, 0:D], zeros[:, :], zeros[:, :], start=False, stop=True).then_inc(g_sum, 1)
            start_counts(pe, again, "p_turned", "pv", "scores")
            slots(pe, lambda j, c: tensor_slot(pe, again, j, c))

        with nc.Block() as block:
            @block.sync
            def _(sp):
                on_flag(sp, sync_again)

            @block.gpsimd
            def _(pool):
                on_flag(pool, pool_again)

            @block.scalar
            def _(act):
                on_flag(act, scalar_again)

            @block.vector
            def _(dve):
                on_flag(dve, vector_again)

            @block.tensor
            def _(pe):
                on_flag(pe, tensor_again)


_INS = ['x', 'adj', 'L0_gnn_W_fwd', 'L0_gnn_W_bwd', 'L0_gnn_W_loop', 'L0_gnn_Wg_fwd', 'L0_gnn_Wg_bwd',
        'L0_gnn_Wg_loop', 'L0_gnn_b_fwd', 'L0_gnn_b_bwd', 'L0_gnn_b_loop', 'L0_gnn_bg_fwd', 'L0_gnn_bg_bwd',
        'L0_gnn_bg_loop', 'L1_gnn_W_w', 'L1_gnn_W_b', 'L1_gnn_Q_w', 'L1_gnn_Q_b', 'L1_gnn_K_w', 'L1_gnn_K_b']


def kernel(**inputs):
    import numpy as _np
    import concourse.bacc as _bacc
    from concourse import mybir as _mybir
    from concourse.bass_utils import run_bass_kernel_spmd as _run

    nc = _bacc.Bacc("TRN2", target_bir_lowering=False, num_devices=1)
    arrays, aps = {}, {}
    for name in _INS:
        arrays[f"in_{name}"] = _np.ascontiguousarray(inputs[name])
        a = arrays[f"in_{name}"]
        aps[name] = nc.dram_tensor(f"in_{name}", a.shape, _mybir.dt.from_np(a.dtype), kind="ExternalInput").ap()
    out = nc.dram_tensor("out", (B, N, D), F32, kind="ExternalOutput").ap()
    build(nc, aps, out)
    r = _run(nc, [arrays], core_ids=[0])
    return r.results[0]["out"]
```

```python
from contextlib import ExitStack

import concourse.bass as bass
from concourse import mybir

F32 = mybir.dt.float32
BF16 = mybir.dt.bfloat16
I32 = mybir.dt.int32
ALU = mybir.AluOpType
ACT = mybir.ActivationFunctionType
AX = mybir.AxisListType

B, N, D = 64, 128, 128
PER = 4
GROUPS = B // PER
W = PER * D
RING = 4
RELS = 39
EPS = 1e-5
SLOPE = 0.2
SCALE = 1.0 / float(D) ** 0.5
MASKED = -(2.0 ** 100)
SPREAD = 32
PLAIN_SUM = 0.25 * W

CONSTANTS = 7


NAMES = (
    "stats0 rstd0 xn0 h0_turned h0T hg tanh vals onehot agg x1 stats1 rstd1 xn1 h1_turned h1T v vT hw hwS "
    "masked scores logits p p_turned pT pv rinv att y counted bn0 bn1 var_eps0 var_eps1 steep extra"
).split()
DMA_NAMES = ("x_in", "adj_in", "y_out")
OPEN = {"p_turned": 1, "pv": 1, "scores": 1, "p": 2, "att": 2, "pT": 1, "rinv": 1, "logits": 1, "y": 2, "y_out": 16}


def semaphores(sem, tag):
    S = {name: sem(f"{tag}_{name}") for name in NAMES}
    return S | {name: [sem(f"{tag}_{name}{r}") for r in range(RING)] for name in DMA_NAMES}


def start_counts(engine, S, *names):
    for name in names:
        for sem in S[name] if name in DMA_NAMES else [S[name]]:
            engine.sem_inc(sem, OPEN[name])


def wait(engine, S, name, value, at=None):
    if isinstance(value, int) and value <= 0:
        return
    engine.wait_ge(S[name] if at is None else S[name][at], value + OPEN.get(name, 0))


def apart(engine, j, passed):
    if not isinstance(j, int):
        engine.sem_inc(passed, 1)


def lin(j, c, per=1, plus=0):
    if isinstance(j, int):
        return per * (4 * j + c) + plus
    k = per * c + plus
    return j * (4 * per) + k if k else j * (4 * per)


def dma_round(j, c):
    r = c // RING + 1
    if isinstance(j, int):
        return 16 * (j + r)
    return j * 16 + 16 * r


def has(j, c):
    return not isinstance(j, int) or 0 <= c < GROUPS


def slots(engine, run, earliest, latest, first=None):
    full = -earliest
    loops = (GROUPS - latest - full) // RING
    for c in range(-latest if first is None else first, full):
        run(0, c)
    with engine.Fori(0, loops, 1) as j:
        for u in range(RING):
            run(j, full + u)
    for c in range(full + RING * loops, GROUPS - earliest):
        run(0, c)


def build(nc, t, out):
    x_dram = t["x"].rearrange("(g b) n d -> g n b d", b=PER)
    adj_dram = t["adj"].rearrange("(g b) n m -> g n b m", b=PER)
    out_dram = out.rearrange("(g b) n d -> g n b d", b=PER)

    with ExitStack() as ctx:
        def sb(name, shape, dt=F32):
            return ctx.enter_context(nc.sbuf_tensor(name, shape, dt))

        def bank(name, cols=512):
            return ctx.enter_context(nc.psum_tensor(name, [128, cols], F32))

        def sem(name):
            return ctx.enter_context(nc.semaphore(name))

        pool_of_tiles = sb("pool_of_tiles", [128, 20 * W])
        tiles = iter(range(20))

        def ring(count):
            return [pool_of_tiles[:, k * W:(k + 1) * W] for k in (next(tiles) for _ in range(count))]

        x = ring(RING)
        adj = [sb(f"adj{r}", [128, W], I32) for r in range(RING)]
        x1 = ring(RING)
        y = ring(RING)
        two = range(2)
        xn0 = ring(2)
        xn1 = ring(2)
        h0T = ring(2)
        h1T = ring(2)
        th = [sb(f"th{r}", [128, W]) for r in two]
        vals = [sb(f"vals{r}", [128, W]) for r in two]
        onehot = [sb(f"onehot{r}", [128, W]) for r in two]
        masked = [sb(f"masked{r}", [128, W], BF16) for r in two]
        vT = [sb(f"vT{r}", [128, W]) for r in two]
        hW = [sb(f"hW{r}", [128, PER, D + 1]) for r in two]
        steep = sb("steep", [128, W])
        logits = [sb(f"logits{r}", [128, W]) for r in two]
        neg_max = [sb(f"neg_max{r}", [128, PER]) for r in two]
        p = [sb(f"p{r}", [128, W]) for r in two]
        p_sum = [sb(f"p_sum{r}", [128, PER]) for r in two]
        rinv = [sb(f"rinv{r}", [128, PER]) for r in two]
        pT = [sb(f"pT{r}", [128, W]) for r in two]
        att = [sb(f"att{r}", [128, W]) for r in two]
        bn = [sb(f"bn{k}", [128, PER, 6]) for k in two]
        mv = [sb(f"mv{k}", [128, PER, 2]) for k in two]
        var_eps = [sb(f"var_eps{k}", [128, PER]) for k in two]
        rstd = [sb(f"rstd{k}", [128, PER]) for k in two]
        counted = sb("counted", [128, GROUPS])
        counted_out = sb("counted_out", [128, W], BF16)

        ident = sb("ident", [128, 128])
        masker = sb("masker", [128, 128], BF16)
        spread = sb("spread", [128, 128], BF16)
        unused = sb("unused", [128, PER])
        minus_half = sb("minus_half", [128, PER])
        W_loop, Wg_loop, Q_w, K_w = (sb(n, [128, 128]) for n in ("W_loop", "Wg_loop", "Q_w", "K_w"))
        W_wb = sb("W_wb", [128, D + 1])
        qk_b = sb("qk_b", [128, 2])
        WgT, QwT, KwT = (sb(n, [128, 128]) for n in ("WgT", "QwT", "KwT"))
        A = sb("A", [128, 128])
        C = sb("C", [128, 128])
        a_col = sb("a_col", [128, 1])
        c_col = sb("c_col", [128, 1])
        w_hg = sb("w_hg", [128, 2 * D])
        w_hw = sb("w_hw", [128, D + 1])
        w_v = sb("w_v", [128, 128])
        v_bias = sb("v_bias", [128, 1])
        rows = sb("rows", [128, 3 * D + 1])
        rest = sb("rest", [128, 3 * D + 1])
        high = sb("high", [128, 3 * D + 1], BF16)
        middle = sb("middle", [128, 3 * D + 1], BF16)
        parts = sb("parts", [128, 3 * D + 1], BF16)
        over = sb("over", [128, GROUPS])
        over_row = sb("over_row", [128, 1])
        flag = sb("flag", [1, 1], I32)

        rel_b = pool_of_tiles[:, 0:RELS * 2 * D].rearrange("p (r k) -> p r k", r=RELS)
        rel_bg = sb("rel_bg", [128, RELS, 2 * D])
        rel_w = sb("rel_w", [128, 4 * D])
        rel_natural = sb("rel_natural", [128, 4 * D])
        rel_WgT = sb("rel_WgT", [128, 2 * D])
        extra = sb("extra", [128, B * D])
        gx = sb("gx", [128, D])
        gadj = sb("gadj", [128, D], I32)
        gbn = sb("gbn", [128, 6])
        gmv = sb("gmv", [128, 2])
        gvar = sb("gvar", [128, 1])
        grstd = sb("grstd", [128, 1])
        gxn = sb("gxn", [128, D])
        ghT = sb("ghT", [128, D])
        adj_both = sb("adj_both", [128, 2 * D])
        ghg = sb("ghg", [128, 4 * D])
        relation = sb("relation", [128, 1])
        gate_in = sb("gate_in", [128, 2 * D])
        gate = sb("gate", [128, 2 * D])
        lifted = sb("lifted", [128, 2 * D])
        gvals = sb("gvals", [128, 2 * D])
        half_hot = sb("half_hot", [128, 2 * D])
        zeros = sb("zeros", [128, D], BF16)
        constants = sem("constants")
        passed = sem("passed")

        b_hg = bank("b_hg", 1024)
        b_e = bank("b_e")
        b_pT = bank("b_pT")
        b_h1 = bank("b_h1")
        b_v = bank("b_v")
        b_agg = bank("b_agg")
        b_pv = bank("b_pv")
        hg_view = b_hg[:, :].rearrange("p (b k) -> p b k", b=PER)

        def graph(tile, b):
            return tile[:, b * D:(b + 1) * D]

        def twice(row):
            return row.unsqueeze(1).to_broadcast([128, 2, row.shape[1]])

        def by_graph(tile):
            return tile[:, :].rearrange("p (b k) -> p b k", b=PER)


        def sync_loads(sp, S, j, c):
            r = c % RING
            wait(sp, S, "x1", lin(j, c, plus=-RING + 1))
            sp.dma_start(x[r][:, :].rearrange("p (b d) -> p b d", b=PER), x_dram[lin(j, c)]).then_inc(S["x_in"][r], 16)
            wait(sp, S, "masked", lin(j, c, plus=-RING + 1))
            wait(sp, S, "counted", lin(j, c, plus=-RING + 1))
            sp.dma_start(adj[r][:, :].rearrange("p (b d) -> p b d", b=PER), adj_dram[lin(j, c)])\
              .then_inc(S["adj_in"][r], 16)

        def sync_store(sp, S, j, c):
            r = c % RING
            wait(sp, S, "y", lin(j, c, plus=1))
            sp.dma_start(out_dram[lin(j, c)], y[r][:, :].rearrange("p (b d) -> p b d", b=PER)).then_inc(S["y_out"][r], 16)

        def sync_program(sp, S, load_weights=None):
            start_counts(sp, S, "y_out")
            behind = RING + 3
            for g in range(2 * RING):
                sync_loads(sp, S, 0, g)
                if g == 0 and load_weights:
                    load_weights(sp)
                if g >= behind:
                    sync_store(sp, S, 0, g - behind)
            with sp.Fori(2, GROUPS // RING, 1) as j:
                for u in range(RING):
                    sync_loads(sp, S, j, u)
                    sync_store(sp, S, j, u - behind)
            for g in range(GROUPS - behind, GROUPS):
                sync_store(sp, S, 0, g)
            for r in range(RING):
                wait(sp, S, "y_out", 16 * GROUPS // RING, r)

        def pool_slot(pool, S, j, c):
            g = c
            if has(j, g):
                r = g % 2
                wait(pool, S, "scores", lin(j, g, plus=-1))
                apart(pool, j, passed)
                pool.tensor_scalar(masked[r][:, :], adj[g % RING][:, :], 0.0, None, ALU.is_equal)\
                    .then_inc(S["masked"], 1)
            g = c + 1
            if has(j, g):
                r = g % 2
                pool.wait_ge(S["adj_in"][g % RING], dma_round(j, g))
                wait(pool, S, "agg", lin(j, g, plus=-1))
                apart(pool, j, passed)
                pool.tensor_scalar(onehot[r][:, :], adj[g % RING][:, :], 1.0, None, ALU.is_equal)\
                    .then_inc(S["onehot"], 1)
            for k, g in ((0, c + 2), (1, c)):
                if has(j, g):
                    pool.wait_ge(S[f"stats{k}"], lin(j, g, plus=1))
                    apart(pool, j, passed)
                    pool.tensor_scalar(var_eps[k][:, :], mv[k][:, :, 1], EPS, None, ALU.add)\
                        .then_inc(S[f"var_eps{k}"], 1)
                    pool.wait_ge(S[f"var_eps{k}"], lin(j, g, plus=1))
                    pool.tensor_tensor(rstd[k][:, :], var_eps[k][:, :], minus_half[:, :], ALU.pow)\
                        .then_inc(S[f"rstd{k}"], 1)
            g = c - 3
            if has(j, g):
                r = g % RING
                wait(pool, S, "att", lin(j, g, plus=1))
                wait(pool, S, "y_out", dma_round(j, g - RING), r)
                pool.tensor_tensor(y[r][:, :], att[g % 2][:, :], x1[r][:, :], ALU.add).then_inc(S["y"], 1)

        def pool_program(pool, S):
            start_counts(pool, S, "y")
            slots(pool, lambda j, c: pool_slot(pool, S, j, c), -3, 2)

        def scalar_slot(act, S, j, c):
            g = c + 1
            if has(j, g):
                r = g % 2
                act.wait_ge(S["h0_turned"], lin(j, g, plus=1))
                wait(act, S, "hg", lin(j, g, plus=-1))
                nc.scalar.activation(h0T[r][:, :], b_v[:, :], ACT.Relu).then_inc(S["h0T"], 1)
            g = c - 1
            if has(j, g):
                r = g % 2
                act.wait_ge(S["h1_turned"], lin(j, g, plus=1))
                wait(act, S, "scores", lin(j, g, plus=-1))
                nc.scalar.activation(h1T[r][:, :], b_h1[:, :], ACT.Relu).then_inc(S["h1T"], 1)
            g = c - 3
            if has(j, g):
                r = g % 2
                wait(act, S, "pv", lin(j, g, plus=1))
                wait(act, S, "rinv", lin(j, g, plus=1))
                wait(act, S, "y", lin(j, g, plus=-1))
                for b in range(PER):
                    ins = nc.scalar.activation(graph(att[r], b), graph(b_pv, b), ACT.Relu, scale=rinv[r][:, b:b + 1])
                ins.then_inc(S["att"], 1)
            g = c - 1
            if has(j, g):
                r = g % 2
                act.wait_ge(S["v"], lin(j, g, plus=1))
                wait(act, S, "scores", lin(j, g, plus=-1))
                nc.scalar.activation(vT[r][:, :], b_v[:, :], ACT.Identity, bias=v_bias[:, 0:1]).then_inc(S["vT"], 1)
            g = c - 1
            if has(j, g):
                act.wait_ge(S["adj_in"][g % RING], dma_round(j, g))
                wait(act, S, "counted", lin(j, g))
                col = lin(j, g)
                at = counted[:, col:col + 1] if isinstance(col, int) else counted[:, bass.ds(col, 1)]
                nc.scalar.activation(counted_out[:, :], adj[g % RING][:, :], ACT.Square, bias=minus_half[:, 0:1],
                                     accum_out=at).then_inc(S["counted"], 1)
            g = c - 1
            if has(j, g):
                r = g % 2
                act.wait_ge(S["hw"], lin(j, g, plus=1))
                wait(act, S, "pv", lin(j, g, plus=-1))
                wait(act, S, "logits", lin(j, g, PER, -PER))
                nc.scalar.activation(hW[r][:, :, :], hg_view[:, :, 0:D + 1], ACT.Copy).then_inc(S["hwS"], 1)
            g = c - 2
            if has(j, g):
                r = g % 2
                wait(act, S, "p_turned", lin(j, g, plus=1))
                wait(act, S, "pv", lin(j, g, plus=-1))
                nc.scalar.activation(pT[r][:, :], b_pT[:, :], ACT.Copy).then_inc(S["pT"], 1)
            g = c - 1
            if has(j, g):
                r = g % 2
                wait(act, S, "p_turned", lin(j, g, plus=-1))
                wait(act, S, "rinv", lin(j, g, plus=-1))
                for b in range(PER):
                    wait(act, S, "logits", lin(j, g, PER, b + 1))
                    ins = nc.scalar.activation(graph(p[r], b), graph(logits[r], b), ACT.Exp,
                                               bias=neg_max[r][:, b:b + 1], scale=-1.0, accum_out=p_sum[r][:, b:b + 1])
                ins.then_inc(S["p"], 1)
            g = c + 1
            if has(j, g):
                r = g % 2
                act.wait_ge(S["hg"], lin(j, g, plus=1))
                wait(act, S, "vals", lin(j, g, plus=-1))
                nc.scalar.activation(by_graph(th[r]), hg_view[:, :, D:2 * D], ACT.Tanh, scale=0.5).then_inc(S["tanh"], 1)

        def norm_stats(dve, S, j, g, tile, k):
            for b in range(PER):
                ins = nc.vector.bn_stats(bn[k][:, b, :], graph(tile, b))
            ins.then_inc(S[f"bn{k}"], 1)
            dve.wait_ge(S[f"bn{k}"], lin(j, g, plus=1))
            apart(dve, j, passed)
            for b in range(PER):
                ins = nc.vector.bn_aggr(mv[k][:, b, :], bn[k][:, b, :])
            ins.then_inc(S[f"stats{k}"], 1)

        def norm_apply(tile_out, tile, k):
            for b in range(PER):
                ins = nc.vector.tensor_scalar(graph(tile_out, b), graph(tile, b), mv[k][:, b, 0:1],
                                              rstd[k][:, b:b + 1], ALU.subtract, ALU.mult)
            return ins

        def first_norm_stats(dve, S, j, g):
            if has(j, g):
                dve.wait_ge(S["x_in"][g % RING], dma_round(j, g))
                norm_stats(dve, S, j, g, x[g % RING], 0)

        def first_norm(dve, S, j, g):
            if has(j, g):
                dve.wait_ge(S["rstd0"], lin(j, g, plus=1))
                wait(dve, S, "h0_turned", lin(j, g, plus=-1))
                norm_apply(xn0[g % 2], x[g % RING], 0).then_inc(S["xn0"], 1)

        def vector_slot(dve, S, j, c, extra=None):
            g = c - 2
            if has(j, g):
                r = g % 2
                wait(dve, S, "p", lin(j, g, plus=-1))
                dve.wait_ge(S["hwS"], lin(j, g, plus=1))
                wait(dve, S, "scores", lin(j, g, plus=1))
                for b in range(PER + 1):
                    if b < PER:
                        
                        nc.vector.tensor_scalar(graph(steep, b), graph(b_e, b), SLOPE - 1.0, hW[r][:, b, D:D + 1],
                                                ALU.mult, ALU.max).then_inc(S["steep"], 1)
                    if b >= 1:
                        dve.wait_ge(S["steep"], lin(j, g, PER, b))
                        apart(dve, j, passed)
                        nc.vector.tensor_tensor_reduce(graph(logits[r], b - 1), graph(b_e, b - 1), graph(steep, b - 1),
                                                       -1.0, 3.0e38, ALU.add, ALU.min,
                                                       neg_max[r][:, b - 1:b]).then_inc(S["logits"], 1)
            g = c - 1
            if has(j, g):
                dve.wait_ge(S["rstd1"], lin(j, g, plus=1))
                wait(dve, S, "h1_turned", lin(j, g, plus=-1))
                norm_apply(xn1[g % 2], x1[g % RING], 1).then_inc(S["xn1"], 1)
            g = c
            if has(j, g):
                r = g % 2
                dve.wait_ge(S["tanh"], lin(j, g, plus=1))
                wait(dve, S, "agg", lin(j, g, plus=-1))
                nc.vector.scalar_tensor_tensor(by_graph(vals[r]), by_graph(th[r]), 1.0, hg_view[:, :, 0:D],
                                               ALU.add, ALU.mult).then_inc(S["vals"], 1)
            first_norm_stats(dve, S, j, c + 2)
            g = c
            if has(j, g):
                r = g % RING
                dve.wait_ge(S["agg"], lin(j, g, plus=1))
                wait(dve, S, "y", lin(j, g, plus=-RING + 1))
                if extra is None:
                    nc.vector.scalar_tensor_tensor(x1[r][:, :], b_agg[:, :], 0.0, x[r][:, :], ALU.max, ALU.add)\
                        .then_inc(S["x1"], 1)
                else:
                    at = lin(j, g, W)
                    more = extra[:, at:at + W] if isinstance(at, int) else extra[:, bass.ds(at, W)]
                    nc.vector.tensor_tensor(steep[:, :], b_agg[:, :], more, ALU.add).then_inc(S["extra"], 1)
                    dve.wait_ge(S["extra"], lin(j, g, plus=1))
                    nc.vector.scalar_tensor_tensor(x1[r][:, :], steep[:, :], 0.0, x[r][:, :], ALU.max, ALU.add)\
                        .then_inc(S["x1"], 1)
            g = c - 2
            if has(j, g):
                r = g % 2
                wait(dve, S, "p", lin(j, g, plus=1))
                wait(dve, S, "att", lin(j, g, plus=-1))
                nc.vector.reciprocal(rinv[r][:, :], p_sum[r][:, :]).then_inc(S["rinv"], 1)
            g = c
            if has(j, g):
                r = g % RING
                dve.wait_ge(S["x1"], lin(j, g, plus=1))
                norm_stats(dve, S, j, g, x1[r], 1)
            first_norm(dve, S, j, c + 2)

        def tensor_slot(pe, S, j, c):
            def turn(bank_, tile):
                for b in range(PER):
                    ins = nc.tensor.transpose(graph(bank_, b), graph(tile, b), ident[:, :])
                return ins

            g = c - 1
            if has(j, g):
                pe.wait_ge(S["xn1"], lin(j, g, plus=1))
                wait(pe, S, "h1T", lin(j, g))
                turn(b_h1, xn1[g % 2]).then_inc(S["h1_turned"], 1)
            g = c - 2
            if has(j, g):
                wait(pe, S, "p", lin(j, g, plus=1))
                wait(pe, S, "pT", lin(j, g))
                turn(b_pT, p[g % 2]).then_inc(S["p_turned"], 1)
            g = c
            if has(j, g):
                r = g % 2
                pe.wait_ge(S["vals"], lin(j, g, plus=1))
                pe.wait_ge(S["onehot"], lin(j, g, plus=1))
                wait(pe, S, "x1", lin(j, g))
                for b in range(PER):
                    ins = nc.tensor.matmul(graph(b_agg, b), graph(onehot[r], b), graph(vals[r], b), start=True, stop=True)
                ins.then_inc(S["agg"], 1)
            g = c - 1
            if has(j, g):
                r = g % 2
                pe.wait_ge(S["h1T"], lin(j, g, plus=1))
                after = lambda k: lin(j, g, plus=k) if not isinstance(j, int) else min(g + k, GROUPS)
                pe.wait_ge(S["h0T"], after(3))
                nc.tensor.matmul(b_v[:, :], w_v[:, :], h1T[r][:, :], start=True, stop=True).then_inc(S["v"], 1)
                pe.wait_ge(S["vals"], after(2))
                for b in range(PER):
                    if b % 2 == 0:
                        nc.tensor.matmul(hg_view[:, b:b + 2, 0:D + 1], spread[:, :], twice(parts[:, 2 * D:3 * D + 1]),
                                         start=True, stop=False)
                    ins = nc.tensor.matmul(hg_view[:, b, 0:D + 1], graph(h1T[r], b), w_hw[:, :], start=False,
                                           stop=b % 2 == 1)
                ins.then_inc(S["hw"], 1)
                pe.wait_ge(S["masked"], lin(j, g, plus=1))
                wait(pe, S, "logits", lin(j, g, PER))
                pe.wait_ge(S["vT"], lin(j, g, plus=1))
                nc.tensor.matmul(b_e[:, :], masker[:, :], masked[r][:, :], start=True, stop=False)
                for b in range(PER):
                    ins = nc.tensor.matmul(graph(b_e, b), graph(vT[r], b), graph(h1T[r], b), start=False,
                                           stop=b == PER - 1)
                ins.then_inc(S["scores"], 1)
            g = c + 1
            if has(j, g):
                r = g % 2
                pe.wait_ge(S["h0T"], lin(j, g, plus=1))
                wait(pe, S, "hwS", lin(j, g, plus=-1))
                for b in range(PER):
                    if b % 2 == 0:
                        nc.tensor.matmul(hg_view[:, b:b + 2, :], spread[:, :], twice(parts[:, 0:2 * D]),
                                         start=True, stop=False)
                    ins = nc.tensor.matmul(hg_view[:, b, :], graph(h0T[r], b), w_hg[:, :], start=False, stop=b % 2 == 1)
                ins.then_inc(S["hg"], 1)
            g = c + 2
            if has(j, g):
                pe.wait_ge(S["xn0"], lin(j, g, plus=1))
                wait(pe, S, "vT", lin(j, g, plus=-2))
                turn(b_v, xn0[g % 2]).then_inc(S["h0_turned"], 1)
            g = c - 2
            if has(j, g):
                r = g % 2
                wait(pe, S, "pT", lin(j, g, plus=1))
                wait(pe, S, "att", lin(j, g))
                for b in range(PER):
                    ins = nc.tensor.matmul(graph(b_pv, b), graph(pT[r], b), hW[r][:, b, 0:D], start=True, stop=True)
                ins.then_inc(S["pv"], 1)


        main = semaphores(sem, "m")
        weights_in = sem("weights_in")
        rows_in = sem("rows_in")
        scores_in = sem("scores_in")
        turned = sem("turned")
        gates_folded = sem("gates_folded")
        scores_folded = sem("scores_folded")
        folded = sem("folded")
        flagged = sem("flagged")
        flag_turned = sem("flag_turned")

        def weight_loads(sp):
            sp.dma_start(W_loop[:, :], t["L0_gnn_W_loop"]).then_inc(weights_in, 16)
            sp.dma_start(Wg_loop[:, :], t["L0_gnn_Wg_loop"]).then_inc(weights_in, 16)
            sp.dma_start(W_wb[:, 0:D], t["L1_gnn_W_w"]).then_inc(scores_in, 16)
            sp.dma_start(Q_w[:, :], t["L1_gnn_Q_w"]).then_inc(scores_in, 16)
            sp.dma_start(K_w[:, :], t["L1_gnn_K_w"]).then_inc(scores_in, 16)
            sp.dma_start(W_wb[:, D:D + 1], t["L1_gnn_W_b"].unsqueeze(1)).then_inc(scores_in, 16)
            sp.dma_start(qk_b[:, 0:1], t["L1_gnn_Q_b"].unsqueeze(1)).then_inc(scores_in, 16)
            sp.dma_start(qk_b[:, 1:2], t["L1_gnn_K_b"].unsqueeze(1)).then_inc(scores_in, 16)

        block = nc.Block()
        with block:
            @block.sync
            def _(sp):
                sync_program(sp, main, weight_loads)

            @block.gpsimd
            def _(pool):
                pool.memset(ident[:, :], 0.0).then_inc(constants, 1)
                pool.memset(masker[:, :], 0.0).then_inc(constants, 1)
                pool.memset(spread[:, :], 1.0 / SPREAD).then_inc(constants, 1)
                pool.memset(minus_half[:, :], -0.5).then_inc(constants, 1)
                pool.memset(parts[:, :], 0.0).then_inc(constants, 1)
                pool.wait_ge(constants, 2)
                for m, fill in ((ident, 1.0), (masker, MASKED)):
                    pool.affine_select(out=m[:, :], in_=m[:, :], compare_op=ALU.not_equal, fill=fill, base=0,
                                       pattern=[[-1, 128]], channel_multiplier=1).then_inc(constants, 1)
                pool.wait_ge(constants, CONSTANTS)
                pool_program(pool, main)

            @block.scalar
            def _(act):
                act.dma_start(rows[:, 0:D], t["L0_gnn_b_loop"].to_broadcast([128, D])).then_inc(rows_in, 16)
                act.dma_start(rows[:, D:2 * D], t["L0_gnn_bg_loop"].to_broadcast([128, D])).then_inc(rows_in, 16)
                act.dma_start(rows[:, 2 * D:3 * D], t["L1_gnn_W_b"].unsqueeze(0).to_broadcast([128, D]))\
                   .then_inc(rows_in, 16)
                act.wait_ge(constants, 4)
                nc.scalar.activation(unused[:, :], minus_half[:, :], ACT.Tanh)
                act.wait_ge(turned, 1)
                nc.scalar.activation(WgT[:, :], b_e[:, D:2 * D], ACT.Copy).then_inc(gates_folded, 1)
                nc.scalar.activation(w_hg[:, 0:D], b_e[:, 0:D], ACT.Copy, scale=0.5)
                act.wait_ge(turned, 2)
                nc.scalar.activation(w_hg[:, D:2 * D], b_agg[:, 0:D], ACT.Copy).then_inc(gates_folded, 1)
                start_counts(act, main, "p", "att", "pT")

                def run(j, c):
                    if isinstance(j, int) and c == 0:
                        act.wait_ge(turned, 4)
                        nc.scalar.activation(A[:, :], b_pv[:, 0:D], ACT.Copy)
                        nc.scalar.activation(C[:, :], b_pv[:, 2 * D:3 * D], ACT.Copy)
                        nc.scalar.activation(a_col[:, :], b_pv[:, D:D + 1], ACT.Identity, bias=qk_b[:, 0:1])
                        nc.scalar.activation(c_col[:, :], b_pv[:, 3 * D:3 * D + 1], ACT.Identity, bias=qk_b[:, 1:2])\
                            .then_inc(scores_folded, 1)
                        act.wait_ge(turned, 5)
                        nc.scalar.activation(rows[:, 3 * D:3 * D + 1], b_pv[:, D + 2:D + 3], ACT.Copy,
                                             scale=SCALE * (1.0 - SLOPE)).then_inc(scores_folded, 1)
                        nc.scalar.activation(w_v[:, :], b_pv[:, 0:D], ACT.Copy, scale=SCALE)
                        nc.scalar.activation(v_bias[:, :], b_pv[:, D:D + 1], ACT.Copy, scale=SCALE)
                        nc.scalar.activation(w_hw[:, D:D + 1], b_pv[:, D + 1:D + 2], ACT.Copy,
                                             scale=SCALE * (1.0 - SLOPE)).then_inc(scores_folded, 1)
                    if isinstance(j, int) and c == 1:
                        act.wait_ge(scores_folded, 3)
                    scalar_slot(act, main, j, c)
                slots(act, run, -3, 1)

            @block.vector
            def _(dve):
                def part_rows(s, count):
                    nc.vector.tensor_copy(high[:, s], rows[:, s]).then_inc(folded, 1)
                    dve.wait_ge(folded, count + 1)
                    nc.vector.tensor_tensor(rest[:, s], rows[:, s], high[:, s], ALU.subtract).then_inc(folded, 1)
                    dve.wait_ge(folded, count + 2)
                    nc.vector.tensor_copy(middle[:, s], rest[:, s]).then_inc(folded, 1)

                def join_rows(s, count):
                    dve.wait_ge(folded, count)
                    nc.vector.tensor_copy(parts[0:32, s], high[0:32, s])
                    nc.vector.tensor_copy(parts[32:64, s], middle[32:64, s])
                    nc.vector.tensor_tensor(parts[64:96, s], rest[64:96, s], middle[64:96, s], ALU.subtract)\
                        .then_inc(folded, 1)

                start_counts(dve, main, "rinv", "logits")
                first_norm_stats(dve, main, 0, 0)
                dve.wait_ge(rows_in, 48)
                nc.vector.tensor_scalar(rows[:, 0:D], rows[:, 0:D], 0.5, None, ALU.mult).then_inc(folded, 1)
                dve.wait_ge(folded, 1)
                part_rows(slice(0, 3 * D), 1)
                first_norm(dve, main, 0, 0)
                dve.wait_ge(constants, CONSTANTS)
                join_rows(slice(0, 3 * D), 4)
                first_norm_stats(dve, main, 0, 1)
                dve.wait_ge(turned, 3)
                nc.vector.tensor_copy(w_hw[:, 0:D], b_pv[:, 0:D])
                nc.vector.tensor_copy(QwT[:, :], b_pv[:, D:2 * D])
                nc.vector.tensor_copy(KwT[:, :], b_pv[:, 2 * D:3 * D]).then_inc(folded, 1)
                first_norm(dve, main, 0, 1)

                def run(j, c):
                    vector_slot(dve, main, j, c)
                    if isinstance(j, int) and c == 0:
                        dve.wait_ge(scores_folded, 2)
                        part_rows(slice(3 * D, 3 * D + 1), 6)
                        join_rows(slice(3 * D, 3 * D + 1), 9)
                    if isinstance(j, int) and c == GROUPS + 1:
                        dve.wait_ge(main["counted"], GROUPS)
                        nc.vector.tensor_scalar(over[:, :], counted[:, :], PLAIN_SUM + 1.0, None, ALU.is_gt)\
                            .then_inc(flagged, 1)
                        dve.wait_ge(flagged, 1)
                        nc.vector.tensor_reduce(over_row[:, :], over[:, :], AX.X, ALU.max).then_inc(flagged, 1)
                slots(dve, run, -2, 2, first=0)
                dve.wait_ge(flag_turned, 1)
                nc.vector.tensor_reduce(flag[:, :], b_agg[0:1, 0:128], AX.X, ALU.max).then_inc(flagged, 1)

            @block.tensor
            def _(pe):
                start_counts(pe, main, "p_turned", "pv", "scores")
                pe.wait_ge(constants, 4)

                def keep_busy(products):
                    for _ in range(products):
                        nc.tensor.matmul(b_h1[:, :].rearrange("p (b k) -> p b k", b=PER), spread[:, :],
                                         spread[:, :].unsqueeze(1).to_broadcast([128, PER, 128]), start=True, stop=True)

                keep_busy(8)
                pe.wait_ge(constants, CONSTANTS)
                pe.wait_ge(weights_in, 32)
                nc.tensor.transpose(b_e[:, 0:D], W_loop[:, :], ident[:, :])
                nc.tensor.transpose(b_e[:, D:2 * D], Wg_loop[:, :], ident[:, :]).then_inc(turned, 1)
                pe.wait_ge(gates_folded, 1)
                nc.tensor.matmul(b_agg[:, 0:D], W_loop[:, :], WgT[:, :], start=True, stop=True).then_inc(turned, 1)
                keep_busy(4)
                tensor_slot(pe, main, 0, -2)
                pe.wait_ge(scores_in, 96)
                nc.tensor.transpose(b_pv[:, 0:D], W_wb[:, 0:D], ident[:, :])
                nc.tensor.transpose(b_pv[:, D:2 * D], Q_w[:, :], ident[:, :])
                nc.tensor.transpose(b_pv[:, 2 * D:3 * D], K_w[:, :], ident[:, :]).then_inc(turned, 1)
                pe.wait_ge(gates_folded, 2)
                pe.wait_ge(folded, 5)
                tensor_slot(pe, main, 0, -1)
                pe.wait_ge(folded, 6)
                nc.tensor.matmul(b_pv[:, 0:D + 1], QwT[:, :], W_wb[:, :], start=True, stop=True)
                nc.tensor.matmul(b_pv[:, 2 * D:3 * D + 1], KwT[:, :], W_wb[:, :], start=True, stop=True)\
                  .then_inc(turned, 1)
                pe.wait_ge(scores_folded, 1)
                nc.tensor.matmul(b_pv[:, 0:D], A[:, :], C[:, :], start=True, stop=True)
                nc.tensor.matmul(b_pv[:, D:D + 1], C[:, :], a_col[:, :], start=True, stop=True)
                nc.tensor.matmul(b_pv[:, D + 1:D + 2], A[:, :], c_col[:, :], start=True, stop=True)
                nc.tensor.matmul(b_pv[:, D + 2:D + 3], a_col[:, 0:1].to_broadcast([128, 128]), c_col[:, :],
                                 start=True, stop=True).then_inc(turned, 1)

                def run(j, c):
                    if isinstance(j, int) and c == 1:
                        pe.wait_ge(scores_folded, 3)
                        pe.wait_ge(folded, 10)
                    tensor_slot(pe, main, j, c)
                slots(pe, run, -2, 2, first=0)
                pe.wait_ge(flagged, 2)
                pe.wait_ge(main["x1"], GROUPS)
                nc.tensor.transpose(b_agg[0:1, 0:128], over_row[:, :], ident[:, :]).then_inc(flag_turned, 1)


        again = semaphores(sem, "a")
        rel_in = sem("rel_in")
        rel_turned = sem("rel_turned")
        rel_folded = sem("rel_folded")
        gx_in = sem("gx_in")
        gadj_in = sem("gadj_in")
        g_bn = sem("g_bn")
        g_stats = sem("g_stats")
        g_var = sem("g_var")
        g_rstd = sem("g_rstd")
        g_xn = sem("g_xn")
        g_turned = sem("g_turned")
        g_hT = sem("g_hT")
        g_hg = sem("g_hg")
        g_ready = sem("g_ready")
        r_gate_in = sem("r_gate_in")
        r_gate = sem("r_gate")
        r_hot = sem("r_hot")
        r_vals = sem("r_vals")
        r_next = sem("r_next")
        r_summed = sem("r_summed")
        g_sum = sem("g_sum")
        g_extra = sem("g_extra")

        def on_flag(engine, program):
            with engine.If(engine.value_load(flag[0:1, 0:1]) > 0):
                program(engine)
                engine.sem_inc(passed, 1)

        def relation_loads(sp, i):
            sp.dma_start(gx[:, :], t["x"][i]).then_inc(gx_in, 16)
            sp.dma_start(gadj[:, :], t["adj"][i]).then_inc(gadj_in, 16)

        def sync_again(sp):
            for k, name in enumerate(("L0_gnn_W_fwd", "L0_gnn_W_bwd", "L0_gnn_Wg_fwd", "L0_gnn_Wg_bwd")):
                sp.dma_start(rel_natural[:, k * D:(k + 1) * D], t[name]).then_inc(rel_in, 16)
            for k, way in enumerate(("fwd", "bwd")):
                for tile, name in ((rel_b, "b"), (rel_bg, "bg")):
                    row = t[f"L0_gnn_{name}_{way}"].unsqueeze(0).to_broadcast([128, RELS, D])
                    sp.dma_start(tile[:, :, k * D:(k + 1) * D], row).then_inc(rel_in, 16)
            relation_loads(sp, 0)
            with sp.Fori(1, B, 1) as i:
                sp.wait_ge(g_xn, i)
                relation_loads(sp, i)
            sp.wait_ge(g_extra, B)
            sync_program(sp, again)

        def pool_again(pool):
            with pool.Fori(0, B, 1) as i:
                pool.wait_ge(g_stats, i + 1)
                pool.sem_inc(passed, 1)
                pool.tensor_scalar(gvar[:, :], gmv[:, 1:2], EPS, None, ALU.add).then_inc(g_var, 1)
                pool.wait_ge(g_var, i + 1)
                pool.tensor_tensor(grstd[:, :], gvar[:, :], minus_half[:, 0:1], ALU.pow).then_inc(g_rstd, 1)
            pool_program(pool, again)

        def scalar_again(act):
            with act.Fori(0, B, 1) as i:
                with act.Fori(0, RELS, 1) as r:
                    act.wait_ge(r_gate_in, i * RELS + r + 1)
                    nc.scalar.activation(gate[:, :], gate_in[:, :], ACT.Tanh, scale=0.5).then_inc(r_gate, 1)
            start_counts(act, again, "p", "att", "pT")
            slots(act, lambda j, c: scalar_slot(act, again, j, c), -3, 1)

        def vector_again(dve):
            nc.vector.memset(zeros[:, :], 0.0).then_inc(rel_folded, 1)
            dve.wait_ge(rel_turned, 1)
            nc.vector.tensor_copy(rel_WgT[:, :], b_e[:, 2 * D:4 * D]).then_inc(rel_folded, 1)
            nc.vector.tensor_copy(rel_w[:, 0:2 * D], b_e[:, 0:2 * D]).then_inc(rel_folded, 1)
            dve.wait_ge(rel_turned, 2)
            nc.vector.tensor_copy(rel_w[:, 2 * D:4 * D], b_pv[:, 0:2 * D]).then_inc(rel_folded, 1)
            dve.wait_ge(rel_in, 16 * 8)
            with dve.Fori(0, B, 1) as i:
                dve.wait_ge(gx_in, i * 16 + 16)
                nc.vector.bn_stats(gbn[:, :], gx[:, :]).then_inc(g_bn, 1)
                dve.wait_ge(g_bn, i + 1)
                dve.sem_inc(passed, 1)
                nc.vector.bn_aggr(gmv[:, :], gbn[:, :]).then_inc(g_stats, 1)
                dve.wait_ge(gadj_in, i * 16 + 16)
                nc.vector.tensor_copy(adj_both[:, D:2 * D], gadj[:, :])
                dve.wait_ge(g_rstd, i + 1)
                nc.vector.tensor_scalar(gxn[:, :], gx[:, :], gmv[:, 0:1], grstd[:, 0:1], ALU.subtract, ALU.mult)\
                    .then_inc(g_xn, 1)
                dve.wait_ge(g_turned, i + 1)
                nc.vector.tensor_scalar(ghT[:, :], b_h1[:, 0:D], 0.0, None, ALU.max)
                nc.vector.tensor_copy(adj_both[:, 0:D], b_h1[:, D:2 * D]).then_inc(g_hT, 1)
                dve.wait_ge(g_hg, i + 1)
                nc.vector.memset(relation[:, :], 2.0)
                nc.vector.tensor_copy(ghg[:, :], b_hg[:, 0:4 * D]).then_inc(g_ready, 1)
                dve.wait_ge(g_ready, i + 1)
                dve.sem_inc(passed, 1)
                with dve.Fori(0, RELS, 1) as r:
                    done = i * RELS + r
                    nc.vector.tensor_tensor(gate_in[:, :], ghg[:, 2 * D:4 * D], rel_bg[:, bass.ds(r, 1), :], ALU.add)\
                        .then_inc(r_gate_in, 1)
                    dve.wait_ge(r_summed, done + 1)
                    nc.vector.tensor_tensor(lifted[:, :], ghg[:, 0:2 * D], rel_b[:, bass.ds(r, 1), :], ALU.add)
                    nc.vector.tensor_scalar(half_hot[:, :], adj_both[:, :], relation[:, 0:1], 0.5, ALU.is_equal,
                                            ALU.mult).then_inc(r_hot, 1)
                    dve.wait_ge(r_hot, done + 1)
                    nc.vector.tensor_scalar(relation[:, :], relation[:, :], 1.0, None, ALU.add).then_inc(r_next, 1)
                    dve.wait_ge(r_gate, done + 1)
                    nc.vector.scalar_tensor_tensor(gvals[:, :], gate[:, :], 1.0, lifted[:, :], ALU.add, ALU.mult)\
                        .then_inc(r_vals, 1)
                    dve.wait_ge(r_next, done + 1)
                dve.wait_ge(g_sum, i + 1)
                nc.vector.tensor_copy(extra[:, bass.ds(i * D, D)], b_agg[:, 0:D]).then_inc(g_extra, 1)
            dve.wait_ge(g_extra, B)
            start_counts(dve, again, "rinv", "logits")
            slots(dve, lambda j, c: vector_slot(dve, again, j, c, extra), -2, 2)

        def tensor_again(pe):
            pe.sem_inc(r_summed, 1)
            pe.wait_ge(rel_in, 16 * 8)
            for k in range(4):
                ins = nc.tensor.transpose(b_e[:, k * D:(k + 1) * D], rel_natural[:, k * D:(k + 1) * D], ident[:, :])
            ins.then_inc(rel_turned, 1)
            pe.wait_ge(rel_folded, 2)
            for k in range(2):
                ins = nc.tensor.matmul(b_pv[:, k * D:(k + 1) * D], rel_natural[:, k * D:(k + 1) * D],
                                       rel_WgT[:, k * D:(k + 1) * D], start=True, stop=True)
            ins.then_inc(rel_turned, 1)
            pe.wait_ge(rel_folded, 4)
            with pe.Fori(0, B, 1) as i:
                pe.wait_ge(g_xn, i + 1)
                nc.tensor.transpose(b_h1[:, 0:D], gxn[:, :], ident[:, :])
                nc.tensor.transpose(b_h1[:, D:2 * D], adj_both[:, D:2 * D], ident[:, :]).then_inc(g_turned, 1)
                pe.wait_ge(g_hT, i + 1)
                nc.tensor.matmul(b_hg[:, 0:4 * D], ghT[:, :], rel_w[:, :], start=True, stop=True).then_inc(g_hg, 1)
                nc.tensor.matmul(b_agg[:, 0:D], zeros[:, :], zeros[:, :], start=True, stop=False)
                with pe.Fori(0, RELS, 1) as r:
                    pe.wait_ge(r_vals, i * RELS + r + 1)
                    for k in range(2):
                        ins = nc.tensor.matmul(b_agg[:, 0:D], half_hot[:, k * D:(k + 1) * D],
                                               gvals[:, k * D:(k + 1) * D], start=False, stop=False)
                    ins.then_inc(r_summed, 1)
                nc.tensor.matmul(b_agg[:, 0:D], zeros[:, :], zeros[:, :], start=False, stop=True).then_inc(g_sum, 1)
            start_counts(pe, again, "p_turned", "pv", "scores")
            slots(pe, lambda j, c: tensor_slot(pe, again, j, c), -2, 2)

        with nc.Block() as block:
            @block.sync
            def _(sp):
                on_flag(sp, sync_again)

            @block.gpsimd
            def _(pool):
                on_flag(pool, pool_again)

            @block.scalar
            def _(act):
                on_flag(act, scalar_again)

            @block.vector
            def _(dve):
                on_flag(dve, vector_again)

            @block.tensor
            def _(pe):
                on_flag(pe, tensor_again)


_INS = ['x', 'adj', 'L0_gnn_W_fwd', 'L0_gnn_W_bwd', 'L0_gnn_W_loop', 'L0_gnn_Wg_fwd', 'L0_gnn_Wg_bwd',
        'L0_gnn_Wg_loop', 'L0_gnn_b_fwd', 'L0_gnn_b_bwd', 'L0_gnn_b_loop', 'L0_gnn_bg_fwd', 'L0_gnn_bg_bwd',
        'L0_gnn_bg_loop', 'L1_gnn_W_w', 'L1_gnn_W_b', 'L1_gnn_Q_w', 'L1_gnn_Q_b', 'L1_gnn_K_w', 'L1_gnn_K_b']


def kernel(**inputs):
    import numpy as _np
    import concourse.bacc as _bacc
    from concourse import mybir as _mybir
    from concourse.bass_utils import run_bass_kernel_spmd as _run

    nc = _bacc.Bacc("TRN2", target_bir_lowering=False, num_devices=1)
    arrays, aps = {}, {}
    for name in _INS:
        arrays[f"in_{name}"] = _np.ascontiguousarray(inputs[name])
        a = arrays[f"in_{name}"]
        aps[name] = nc.dram_tensor(f"in_{name}", a.shape, _mybir.dt.from_np(a.dtype), kind="ExternalInput").ap()
    out = nc.dram_tensor("out", (B, N, D), F32, kind="ExternalOutput").ap()
    build(nc, aps, out)
    r = _run(nc, [arrays], core_ids=[0])
    return r.results[0]["out"]
```

```python
from contextlib import ExitStack

import concourse.bass as bass
from concourse import mybir

F32 = mybir.dt.float32
BF16 = mybir.dt.bfloat16
I32 = mybir.dt.int32
ALU = mybir.AluOpType
ACT = mybir.ActivationFunctionType
AX = mybir.AxisListType

B, N, D = 64, 128, 128
PER = 4
GROUPS = B // PER
W = PER * D
RING = 4
RELS = 39
EPS = 1e-5
SLOPE = 0.2
SCALE = 1.0 / float(D) ** 0.5
MASKED = -(2.0 ** 100)
SPREAD = 32
PLAIN_SUM = 0.25 * W

CONSTANTS = 7

NAMES = (
    "stats0 rstd0 xn0 h0_turned h0T hg tanh vals onehot agg x1 stats1 rstd1 xn1 h1_turned h1T v vT hw hwS "
    "masked scores logits p p_turned pT pv rinv att y counted bn0 bn1 var_eps0 var_eps1 steep extra att_half y_half"
).split()
DMA_NAMES = ("x_in", "adj_in", "y_out")
OPEN = {"p_turned": 1, "pv": 1, "scores": 1, "p": 2, "att": 2, "pT": 1, "rinv": 1, "logits": 1, "y": 2, "y_out": 16}


def semaphores(sem, tag):
    S = {name: sem(f"{tag}_{name}") for name in NAMES}
    return S | {name: [sem(f"{tag}_{name}{r}") for r in range(RING)] for name in DMA_NAMES}


def start_counts(engine, S, *names):
    for name in names:
        for sem in S[name] if name in DMA_NAMES else [S[name]]:
            engine.sem_inc(sem, OPEN[name])


def wait(engine, S, name, value, at=None):
    if isinstance(value, int) and value <= 0:
        return
    engine.wait_ge(S[name] if at is None else S[name][at], value + OPEN.get(name, 0))


def apart(engine, j, passed):
    if not isinstance(j, int):
        engine.sem_inc(passed, 1)


def lin(j, c, per=1, plus=0):
    if isinstance(j, int):
        return per * (4 * j + c) + plus
    k = per * c + plus
    return j * (4 * per) + k if k else j * (4 * per)


def dma_round(j, c):
    r = c // RING + 1
    if isinstance(j, int):
        return 16 * (j + r)
    return j * 16 + 16 * r


def has(j, c):
    return not isinstance(j, int) or 0 <= c < GROUPS


def is_last(j, g):
    return isinstance(j, int) and g == GROUPS - 1


def ends(j, c, after):
    return isinstance(j, int) and c == GROUPS - 1 + after


def slots(engine, run, earliest, latest, first=None):
    full = -earliest
    loops = (GROUPS - latest - full) // RING
    for c in range(-latest if first is None else first, full):
        run(0, c)
    with engine.Fori(0, loops, 1) as j:
        for u in range(RING):
            run(j, full + u)
    for c in range(full + RING * loops, GROUPS - earliest):
        run(0, c)


def build(nc, t, out):
    x_dram = t["x"].rearrange("(g b) n d -> g n b d", b=PER)
    adj_dram = t["adj"].rearrange("(g b) n m -> g n b m", b=PER)
    out_dram = out.rearrange("(g b) n d -> g n b d", b=PER)

    with ExitStack() as ctx:
        def sb(name, shape, dt=F32):
            return ctx.enter_context(nc.sbuf_tensor(name, shape, dt))

        def bank(name, cols=512):
            return ctx.enter_context(nc.psum_tensor(name, [128, cols], F32))

        def sem(name):
            return ctx.enter_context(nc.semaphore(name))

        pool_of_tiles = sb("pool_of_tiles", [128, 20 * W])
        tiles = iter(range(20))

        def ring(count):
            return [pool_of_tiles[:, k * W:(k + 1) * W] for k in (next(tiles) for _ in range(count))]

        x = ring(RING)
        adj = [sb(f"adj{r}", [128, W], I32) for r in range(RING)]
        x1 = ring(RING)
        y = ring(RING)
        two = range(2)
        xn0 = ring(2)
        xn1 = ring(2)
        h0T = ring(2)
        h1T = ring(2)
        th = [sb(f"th{r}", [128, W]) for r in two]
        vals = [sb(f"vals{r}", [128, W]) for r in two]
        onehot = [sb(f"onehot{r}", [128, W]) for r in two]
        masked = [sb(f"masked{r}", [128, W], BF16) for r in two]
        vT = [sb(f"vT{r}", [128, W]) for r in two]
        hW = [sb(f"hW{r}", [128, PER, D + 1]) for r in two]
        steep = sb("steep", [128, W])
        logits = [sb(f"logits{r}", [128, W]) for r in two]
        neg_max = [sb(f"neg_max{r}", [128, PER]) for r in two]
        p = [sb(f"p{r}", [128, W]) for r in two]
        p_sum = [sb(f"p_sum{r}", [128, PER]) for r in two]
        rinv = [sb(f"rinv{r}", [128, PER]) for r in two]
        pT = [sb(f"pT{r}", [128, W]) for r in two]
        att = [sb(f"att{r}", [128, W]) for r in two]
        bn = [sb(f"bn{k}", [128, PER, 6]) for k in two]
        mv = [sb(f"mv{k}", [128, PER, 2]) for k in two]
        var_eps = [sb(f"var_eps{k}", [128, PER]) for k in two]
        rstd = [sb(f"rstd{k}", [128, PER]) for k in two]
        counted = sb("counted", [128, GROUPS])
        counted_out = sb("counted_out", [128, W], BF16)

        ident = sb("ident", [128, 128])
        masker = sb("masker", [128, 128], BF16)
        spread = sb("spread", [128, 128], BF16)
        unused = sb("unused", [128, PER])
        minus_half = sb("minus_half", [128, PER])
        W_loop, Wg_loop, Q_w, K_w = (sb(n, [128, 128]) for n in ("W_loop", "Wg_loop", "Q_w", "K_w"))
        W_wb = sb("W_wb", [128, D + 1])
        qk_b = sb("qk_b", [128, 2])
        WgT, QwT, KwT = (sb(n, [128, 128]) for n in ("WgT", "QwT", "KwT"))
        A = sb("A", [128, 128])
        C = sb("C", [128, 128])
        a_col = sb("a_col", [128, 1])
        c_col = sb("c_col", [128, 1])
        w_hg = sb("w_hg", [128, 2 * D])
        w_hw = sb("w_hw", [128, D + 1])
        w_v = sb("w_v", [128, 128])
        v_bias = sb("v_bias", [128, 1])
        rows = sb("rows", [128, 3 * D + 1])
        rest = sb("rest", [128, 3 * D + 1])
        high = sb("high", [128, 3 * D + 1], BF16)
        middle = sb("middle", [128, 3 * D + 1], BF16)
        parts = sb("parts", [128, 3 * D + 1], BF16)
        over = sb("over", [128, GROUPS])
        over_row = sb("over_row", [128, 1])
        flag = sb("flag", [1, 1], I32)

        rel_b = pool_of_tiles[:, 0:RELS * 2 * D].rearrange("p (r k) -> p r k", r=RELS)
        rel_bg = sb("rel_bg", [128, RELS, 2 * D])
        rel_w = sb("rel_w", [128, 4 * D])
        rel_natural = sb("rel_natural", [128, 4 * D])
        rel_WgT = sb("rel_WgT", [128, 2 * D])
        extra = sb("extra", [128, B * D])
        gx = sb("gx", [128, D])
        gadj = sb("gadj", [128, D], I32)
        gbn = sb("gbn", [128, 6])
        gmv = sb("gmv", [128, 2])
        gvar = sb("gvar", [128, 1])
        grstd = sb("grstd", [128, 1])
        gxn = sb("gxn", [128, D])
        ghT = sb("ghT", [128, D])
        adj_both = sb("adj_both", [128, 2 * D])
        ghg = sb("ghg", [128, 4 * D])
        relation = sb("relation", [128, 1])
        gate_in = sb("gate_in", [128, 2 * D])
        gate = sb("gate", [128, 2 * D])
        lifted = sb("lifted", [128, 2 * D])
        gvals = sb("gvals", [128, 2 * D])
        half_hot = sb("half_hot", [128, 2 * D])
        zeros = sb("zeros", [128, D], BF16)
        constants = sem("constants")
        passed = sem("passed")

        b_hg = bank("b_hg", 1024)
        b_e = bank("b_e")
        b_pT = bank("b_pT")
        b_h1 = bank("b_h1")
        b_v = bank("b_v")
        b_agg = bank("b_agg")
        b_pv = bank("b_pv")
        hg_view = b_hg[:, :].rearrange("p (b k) -> p b k", b=PER)

        def graph(tile, b):
            return tile[:, b * D:(b + 1) * D]

        def twice(row):
            return row.unsqueeze(1).to_broadcast([128, 2, row.shape[1]])

        def by_graph(tile):
            return tile[:, :].rearrange("p (b k) -> p b k", b=PER)


        def load_x(sp, S, j, c):
            r = c % RING
            wait(sp, S, "x1", lin(j, c, plus=-RING + 1))
            sp.dma_start(x[r][:, :].rearrange("p (b d) -> p b d", b=PER), x_dram[lin(j, c)]).then_inc(S["x_in"][r], 16)

        def load_adj(sp, S, j, c):
            r = c % RING
            wait(sp, S, "masked", lin(j, c, plus=-RING + 1))
            wait(sp, S, "counted", lin(j, c, plus=-RING + 1))
            sp.dma_start(adj[r][:, :].rearrange("p (b d) -> p b d", b=PER), adj_dram[lin(j, c)])\
              .then_inc(S["adj_in"][r], 16)

        def sync_store(sp, S, j, c):
            r = c % RING
            wait(sp, S, "y", lin(j, c, plus=1))
            sp.dma_start(out_dram[lin(j, c)], y[r][:, :].rearrange("p (b d) -> p b d", b=PER)).then_inc(S["y_out"][r], 16)

        def store_last(sp, S):
            g = GROUPS - 1
            r = g % RING
            for half in range(2):
                sp.wait_ge(S["y_half"], half + 1)
                two_graphs = slice(half * PER // 2, (half + 1) * PER // 2)
                sp.dma_start(out_dram[g][:, two_graphs, :], by_graph(y[r])[:, two_graphs, :]).then_inc(S["y_out"][r], 16)

        def sync_program(sp, S, weights=False):
            start_counts(sp, S, "y_out")
            behind = RING + 3
            load_x(sp, S, 0, 0)
            if weights:
                load_weights(sp)
            load_x(sp, S, 0, 1)
            load_adj(sp, S, 0, 0)
            if weights:
                load_biases(sp)
            load_adj(sp, S, 0, 1)
            for g in range(2, 2 * RING):
                load_x(sp, S, 0, g)
                load_adj(sp, S, 0, g)
                if g >= behind:
                    sync_store(sp, S, 0, g - behind)
            with sp.Fori(2, GROUPS // RING, 1) as j:
                for u in range(RING):
                    load_x(sp, S, j, u)
                    load_adj(sp, S, j, u)
                    sync_store(sp, S, j, u - behind)
            for g in range(GROUPS - behind, GROUPS - 1):
                sync_store(sp, S, 0, g)
            store_last(sp, S)
            for r in range(RING):
                stores = GROUPS // RING + (1 if r == (GROUPS - 1) % RING else 0)
                wait(sp, S, "y_out", 16 * stores, r)

        def mask(pool, S, j, g):
            if has(j, g):
                r = g % 2
                wait(pool, S, "scores", lin(j, g, plus=-1))
                apart(pool, j, passed)
                pool.tensor_scalar(masked[r][:, :], adj[g % RING][:, :], 0.0, None, ALU.is_equal)\
                    .then_inc(S["masked"], 1)

        def one_hot(pool, S, j, g):
            if has(j, g):
                r = g % 2
                pool.wait_ge(S["adj_in"][g % RING], dma_round(j, g))
                wait(pool, S, "agg", lin(j, g, plus=-1))
                apart(pool, j, passed)
                pool.tensor_scalar(onehot[r][:, :], adj[g % RING][:, :], 1.0, None, ALU.is_equal)\
                    .then_inc(S["onehot"], 1)

        def add_attention(pool, S, j, g):
            if has(j, g):
                r = g % RING
                wait(pool, S, "att", lin(j, g, plus=1))
                wait(pool, S, "y_out", dma_round(j, g - RING), r)
                pool.tensor_tensor(y[r][:, :], att[g % 2][:, :], x1[r][:, :], ALU.add).then_inc(S["y"], 1)

        def inverse_deviation(pool, S, j, g, k):
            if has(j, g):
                pool.wait_ge(S[f"stats{k}"], lin(j, g, plus=1))
                apart(pool, j, passed)
                pool.tensor_scalar(var_eps[k][:, :], mv[k][:, :, 1], EPS, None, ALU.add)\
                    .then_inc(S[f"var_eps{k}"], 1)
                pool.wait_ge(S[f"var_eps{k}"], lin(j, g, plus=1))
                pool.tensor_tensor(rstd[k][:, :], var_eps[k][:, :], minus_half[:, :], ALU.pow)\
                    .then_inc(S[f"rstd{k}"], 1)

        def pool_slot(pool, S, j, c):
            mask(pool, S, j, c)
            one_hot(pool, S, j, c + 1)
            inverse_deviation(pool, S, j, c + 2, 0)
            inverse_deviation(pool, S, j, c, 1)
            if not is_last(j, c - 3):
                add_attention(pool, S, j, c - 3)

        def pool_program(pool, S):
            start_counts(pool, S, "y")
            slots(pool, lambda j, c: pool_slot(pool, S, j, c), -3, 2)

        def relu_first(act, S, j, g):
            if has(j, g):
                r = g % 2
                act.wait_ge(S["h0_turned"], lin(j, g, plus=1))
                wait(act, S, "hg", lin(j, g, plus=-1))
                nc.scalar.activation(h0T[r][:, :], b_v[:, :], ACT.Relu).then_inc(S["h0T"], 1)

        def relu_second(act, S, j, g):
            if has(j, g):
                r = g % 2
                act.wait_ge(S["h1_turned"], lin(j, g, plus=1))
                wait(act, S, "scores", lin(j, g, plus=-1))
                nc.scalar.activation(h1T[r][:, :], b_h1[:, :], ACT.Relu).then_inc(S["h1T"], 1)

        def sum_bank(j, g):
            return b_v if is_last(j, g) else b_pv

        def attention(act, S, j, g):
            if has(j, g):
                r = g % 2
                wait(act, S, "pv", lin(j, g, plus=1))
                wait(act, S, "rinv", lin(j, g, plus=1))
                wait(act, S, "y", lin(j, g, plus=-1))
                for b in range(PER):
                    ins = nc.scalar.activation(graph(att[r], b), graph(sum_bank(j, g), b), ACT.Relu,
                                               scale=rinv[r][:, b:b + 1])
                    if is_last(j, g) and b % 2 == 1:
                        ins.then_inc(S["att_half"], 1)
                if not is_last(j, g):
                    ins.then_inc(S["att"], 1)

        def v_to_sbuf(act, S, j, g):
            if has(j, g):
                r = g % 2
                act.wait_ge(S["v"], lin(j, g, plus=1))
                wait(act, S, "scores", lin(j, g, plus=-1))
                nc.scalar.activation(vT[r][:, :], b_v[:, :], ACT.Identity, bias=v_bias[:, 0:1]).then_inc(S["vT"], 1)

        def count_plain(act, S, j, g):
            if has(j, g):
                act.wait_ge(S["adj_in"][g % RING], dma_round(j, g))
                wait(act, S, "counted", lin(j, g))
                col = lin(j, g)
                at = counted[:, col:col + 1] if isinstance(col, int) else counted[:, bass.ds(col, 1)]
                nc.scalar.activation(counted_out[:, :], adj[g % RING][:, :], ACT.Square, bias=minus_half[:, 0:1],
                                     accum_out=at).then_inc(S["counted"], 1)

        def hw_to_sbuf(act, S, j, g):
            if has(j, g):
                r = g % 2
                act.wait_ge(S["hw"], lin(j, g, plus=1))
                wait(act, S, "pv", lin(j, g, plus=-1))
                wait(act, S, "logits", lin(j, g, PER, -PER))
                nc.scalar.activation(hW[r][:, :, :], hg_view[:, :, 0:D + 1], ACT.Copy).then_inc(S["hwS"], 1)

        def pT_to_sbuf(act, S, j, g):
            if has(j, g):
                r = g % 2
                wait(act, S, "p_turned", lin(j, g, plus=1))
                wait(act, S, "pv", lin(j, g, plus=-1))
                nc.scalar.activation(pT[r][:, :], b_pT[:, :], ACT.Copy).then_inc(S["pT"], 1)

        def exponentials(act, S, j, g):
            if has(j, g):
                r = g % 2
                wait(act, S, "p_turned", lin(j, g, plus=-1))
                wait(act, S, "rinv", lin(j, g, plus=-1))
                for b in range(PER):
                    wait(act, S, "logits", lin(j, g, PER, b + 1))
                    ins = nc.scalar.activation(graph(p[r], b), graph(logits[r], b), ACT.Exp,
                                               bias=neg_max[r][:, b:b + 1], scale=-1.0, accum_out=p_sum[r][:, b:b + 1])
                ins.then_inc(S["p"], 1)

        def gate_tanh(act, S, j, g):
            if has(j, g):
                r = g % 2
                act.wait_ge(S["hg"], lin(j, g, plus=1))
                wait(act, S, "vals", lin(j, g, plus=-1))
                nc.scalar.activation(by_graph(th[r]), hg_view[:, :, D:2 * D], ACT.Tanh, scale=0.5).then_inc(S["tanh"], 1)

        def scalar_slot(act, S, j, c):
            if ends(j, c, 1):
                attention(act, S, j, c - 3)
                relu_second(act, S, j, c - 1)
                exponentials(act, S, j, c - 2)
                v_to_sbuf(act, S, j, c - 1)
                hw_to_sbuf(act, S, j, c - 1)
                pT_to_sbuf(act, S, j, c - 2)
                count_plain(act, S, j, c - 1)
                exponentials(act, S, j, c - 1)
                return
            if ends(j, c, 2):
                pT_to_sbuf(act, S, j, c - 2)
                attention(act, S, j, c - 3)
                return
            relu_first(act, S, j, c + 1)
            relu_second(act, S, j, c - 1)
            attention(act, S, j, c - 3)
            v_to_sbuf(act, S, j, c - 1)
            count_plain(act, S, j, c - 1)
            hw_to_sbuf(act, S, j, c - 1)
            pT_to_sbuf(act, S, j, c - 2)
            if not ends(j, c, 0):
                exponentials(act, S, j, c - 1)
            gate_tanh(act, S, j, c + 1)

        def norm_stats(dve, S, j, g, tile, k):
            for b in range(PER):
                ins = nc.vector.bn_stats(bn[k][:, b, :], graph(tile, b))
            ins.then_inc(S[f"bn{k}"], 1)
            dve.wait_ge(S[f"bn{k}"], lin(j, g, plus=1))
            apart(dve, j, passed)
            for b in range(PER):
                ins = nc.vector.bn_aggr(mv[k][:, b, :], bn[k][:, b, :])
            ins.then_inc(S[f"stats{k}"], 1)

        def norm_apply(tile_out, tile, k):
            for b in range(PER):
                ins = nc.vector.tensor_scalar(graph(tile_out, b), graph(tile, b), mv[k][:, b, 0:1],
                                              rstd[k][:, b:b + 1], ALU.subtract, ALU.mult)
            return ins

        def first_norm_stats(dve, S, j, g):
            if has(j, g):
                dve.wait_ge(S["x_in"][g % RING], dma_round(j, g))
                norm_stats(dve, S, j, g, x[g % RING], 0)

        def first_norm(dve, S, j, g):
            if has(j, g):
                dve.wait_ge(S["rstd0"], lin(j, g, plus=1))
                wait(dve, S, "h0_turned", lin(j, g, plus=-1))
                norm_apply(xn0[g % 2], x[g % RING], 0).then_inc(S["xn0"], 1)

        def second_norm(dve, S, j, g):
            if has(j, g):
                dve.wait_ge(S["rstd1"], lin(j, g, plus=1))
                wait(dve, S, "h1_turned", lin(j, g, plus=-1))
                norm_apply(xn1[g % 2], x1[g % RING], 1).then_inc(S["xn1"], 1)

        def scores_to_logits(dve, S, j, g):
            if has(j, g):
                r = g % 2
                wait(dve, S, "p", lin(j, g, plus=-1))
                dve.wait_ge(S["hwS"], lin(j, g, plus=1))
                wait(dve, S, "scores", lin(j, g, plus=1))
                for b in range(PER + 1):
                    if b < PER:
                        nc.vector.tensor_scalar(graph(steep, b), graph(b_e, b), SLOPE - 1.0, hW[r][:, b, D:D + 1],
                                                ALU.mult, ALU.max).then_inc(S["steep"], 1)
                    if b >= 1:
                        dve.wait_ge(S["steep"], lin(j, g, PER, b))
                        apart(dve, j, passed)
                        nc.vector.tensor_tensor_reduce(graph(logits[r], b - 1), graph(b_e, b - 1), graph(steep, b - 1),
                                                       -1.0, 3.0e38, ALU.add, ALU.min,
                                                       neg_max[r][:, b - 1:b]).then_inc(S["logits"], 1)

        def gated_values(dve, S, j, g):
            if has(j, g):
                r = g % 2
                dve.wait_ge(S["tanh"], lin(j, g, plus=1))
                wait(dve, S, "agg", lin(j, g, plus=-1))
                nc.vector.scalar_tensor_tensor(by_graph(vals[r]), by_graph(th[r]), 1.0, hg_view[:, :, 0:D],
                                               ALU.add, ALU.mult).then_inc(S["vals"], 1)

        def residual(dve, S, j, g, extra=None):
            if has(j, g):
                r = g % RING
                dve.wait_ge(S["agg"], lin(j, g, plus=1))
                wait(dve, S, "y", lin(j, g, plus=-RING + 1))
                if extra is None:
                    nc.vector.scalar_tensor_tensor(x1[r][:, :], b_agg[:, :], 0.0, x[r][:, :], ALU.max, ALU.add)\
                        .then_inc(S["x1"], 1)
                else:
                    at = lin(j, g, W)
                    more = extra[:, at:at + W] if isinstance(at, int) else extra[:, bass.ds(at, W)]
                    nc.vector.tensor_tensor(steep[:, :], b_agg[:, :], more, ALU.add).then_inc(S["extra"], 1)
                    dve.wait_ge(S["extra"], lin(j, g, plus=1))
                    nc.vector.scalar_tensor_tensor(x1[r][:, :], steep[:, :], 0.0, x[r][:, :], ALU.max, ALU.add)\
                        .then_inc(S["x1"], 1)

        def invert_sums(dve, S, j, g):
            if has(j, g):
                r = g % 2
                wait(dve, S, "p", lin(j, g, plus=1))
                wait(dve, S, "att", lin(j, g, plus=-1))
                nc.vector.reciprocal(rinv[r][:, :], p_sum[r][:, :]).then_inc(S["rinv"], 1)

        def second_norm_stats(dve, S, j, g):
            if has(j, g):
                r = g % RING
                dve.wait_ge(S["x1"], lin(j, g, plus=1))
                norm_stats(dve, S, j, g, x1[r], 1)

        def add_last_attention(dve, S):
            g = GROUPS - 1
            r = g % RING
            wait(dve, S, "y_out", dma_round(0, g - RING), r)
            for half in range(2):
                dve.wait_ge(S["att_half"], half + 1)
                s = slice(half * W // 2, (half + 1) * W // 2)
                nc.vector.tensor_tensor(y[r][:, s], att[g % 2][:, s], x1[r][:, s], ALU.add).then_inc(S["y_half"], 1)

        def vector_slot(dve, S, j, c, extra=None):
            if ends(j, c, 1):
                second_norm(dve, S, j, c - 1)
                scores_to_logits(dve, S, j, c - 2)
            else:
                scores_to_logits(dve, S, j, c - 2)
                second_norm(dve, S, j, c - 1)
            gated_values(dve, S, j, c)
            first_norm_stats(dve, S, j, c + 2)
            residual(dve, S, j, c, extra)
            invert_sums(dve, S, j, c - 2)
            second_norm_stats(dve, S, j, c)
            first_norm(dve, S, j, c + 2)
            if ends(j, c, 2):
                add_last_attention(dve, S)

        def turn(bank_, tile):
            for b in range(PER):
                ins = nc.tensor.transpose(graph(bank_, b), graph(tile, b), ident[:, :])
            return ins

        def keep_busy(products):
            for _ in range(products):
                nc.tensor.matmul(b_h1[:, :].rearrange("p (b k) -> p b k", b=PER), spread[:, :],
                                 spread[:, :].unsqueeze(1).to_broadcast([128, PER, 128]), start=True, stop=True)

        def gates_products(pe, S, j, g):
            if has(j, g):
                r = g % 2
                pe.wait_ge(S["h0T"], lin(j, g, plus=1))
                wait(pe, S, "hwS", lin(j, g, plus=-1))
                for b in range(PER):
                    if b % 2 == 0:
                        nc.tensor.matmul(hg_view[:, b:b + 2, :], spread[:, :], twice(parts[:, 0:2 * D]),
                                         start=True, stop=False)
                    ins = nc.tensor.matmul(hg_view[:, b, :], graph(h0T[r], b), w_hg[:, :], start=False, stop=b % 2 == 1)
                ins.then_inc(S["hg"], 1)

        def turn_first_norm(pe, S, j, g):
            if has(j, g):
                pe.wait_ge(S["xn0"], lin(j, g, plus=1))
                wait(pe, S, "vT", lin(j, g, plus=-2))
                turn(b_v, xn0[g % 2]).then_inc(S["h0_turned"], 1)

        def turn_second_norm(pe, S, j, g):
            if has(j, g):
                pe.wait_ge(S["xn1"], lin(j, g, plus=1))
                wait(pe, S, "h1T", lin(j, g))
                turn(b_h1, xn1[g % 2]).then_inc(S["h1_turned"], 1)

        def turn_p(pe, S, j, g):
            if has(j, g):
                wait(pe, S, "p", lin(j, g, plus=1))
                wait(pe, S, "pT", lin(j, g))
                turn(b_pT, p[g % 2]).then_inc(S["p_turned"], 1)

        def relational_sum(pe, S, j, g):
            if has(j, g):
                r = g % 2
                pe.wait_ge(S["vals"], lin(j, g, plus=1))
                pe.wait_ge(S["onehot"], lin(j, g, plus=1))
                wait(pe, S, "x1", lin(j, g))
                for b in range(PER):
                    ins = nc.tensor.matmul(graph(b_agg, b), graph(onehot[r], b), graph(vals[r], b), start=True, stop=True)
                ins.then_inc(S["agg"], 1)

        def v_product(pe, S, j, g):
            if has(j, g):
                r = g % 2
                pe.wait_ge(S["h1T"], lin(j, g, plus=1))
                pe.wait_ge(S["h0T"], lin(j, g, plus=3) if not isinstance(j, int) else min(g + 3, GROUPS))
                nc.tensor.matmul(b_v[:, :], w_v[:, :], h1T[r][:, :], start=True, stop=True).then_inc(S["v"], 1)

        def hw_product(pe, S, j, g):
            if has(j, g):
                r = g % 2
                pe.wait_ge(S["vals"], lin(j, g, plus=2) if not isinstance(j, int) else min(g + 2, GROUPS))
                for b in range(PER):
                    if b % 2 == 0:
                        nc.tensor.matmul(hg_view[:, b:b + 2, 0:D + 1], spread[:, :], twice(parts[:, 2 * D:3 * D + 1]),
                                         start=True, stop=False)
                    ins = nc.tensor.matmul(hg_view[:, b, 0:D + 1], graph(h1T[r], b), w_hw[:, :], start=False,
                                           stop=b % 2 == 1)
                ins.then_inc(S["hw"], 1)

        def scores_product(pe, S, j, g):
            if has(j, g):
                r = g % 2
                pe.wait_ge(S["masked"], lin(j, g, plus=1))
                wait(pe, S, "logits", lin(j, g, PER))
                pe.wait_ge(S["vT"], lin(j, g, plus=1))
                nc.tensor.matmul(b_e[:, :], masker[:, :], masked[r][:, :], start=True, stop=False)
                for b in range(PER):
                    ins = nc.tensor.matmul(graph(b_e, b), graph(vT[r], b), graph(h1T[r], b), start=False,
                                           stop=b == PER - 1)
                ins.then_inc(S["scores"], 1)

        def weighted_sum(pe, S, j, g):
            if has(j, g):
                r = g % 2
                wait(pe, S, "pT", lin(j, g, plus=1))
                if not is_last(j, g):
                    wait(pe, S, "att", lin(j, g))
                for b in range(PER):
                    ins = nc.tensor.matmul(graph(sum_bank(j, g), b), graph(pT[r], b), hW[r][:, b, 0:D], start=True, stop=True)
                ins.then_inc(S["pv"], 1)

        def tensor_slot(pe, S, j, c):
            if ends(j, c, 1):
                turn_second_norm(pe, S, j, c - 1)
                v_product(pe, S, j, c - 1)
                hw_product(pe, S, j, c - 1)
                turn_p(pe, S, j, c - 2)
                scores_product(pe, S, j, c - 1)
                weighted_sum(pe, S, j, c - 2)
                keep_busy(6)
                return
            turn_second_norm(pe, S, j, c - 1)
            turn_p(pe, S, j, c - 2)
            if ends(j, c, 2):
                keep_busy(4)
            relational_sum(pe, S, j, c)
            v_product(pe, S, j, c - 1)
            hw_product(pe, S, j, c - 1)
            scores_product(pe, S, j, c - 1)
            gates_products(pe, S, j, c + 1)
            turn_first_norm(pe, S, j, c + 2)
            weighted_sum(pe, S, j, c - 2)


        main = semaphores(sem, "m")
        weights_in = sem("weights_in")
        rows_in = sem("rows_in")
        products_in = sem("products_in")
        scores_in = sem("scores_in")
        turned = sem("turned")
        gates_folded = sem("gates_folded")
        scores_folded = sem("scores_folded")
        folded = sem("folded")
        flagged = sem("flagged")
        flag_turned = sem("flag_turned")

        def load_weights(sp):
            sp.dma_start(W_loop[:, :], t["L0_gnn_W_loop"]).then_inc(weights_in, 16)
            sp.dma_start(Wg_loop[:, :], t["L0_gnn_Wg_loop"]).then_inc(weights_in, 16)
            sp.dma_start(W_wb[:, 0:D], t["L1_gnn_W_w"]).then_inc(products_in, 16)
            sp.dma_start(Q_w[:, :], t["L1_gnn_Q_w"]).then_inc(products_in, 16)
            sp.dma_start(K_w[:, :], t["L1_gnn_K_w"]).then_inc(products_in, 16)

        def load_biases(sp):
            sp.dma_start(W_wb[:, D:D + 1], t["L1_gnn_W_b"].unsqueeze(1)).then_inc(scores_in, 16)
            sp.dma_start(qk_b[:, 0:1], t["L1_gnn_Q_b"].unsqueeze(1)).then_inc(scores_in, 16)
            sp.dma_start(qk_b[:, 1:2], t["L1_gnn_K_b"].unsqueeze(1)).then_inc(scores_in, 16)

        block = nc.Block()
        with block:
            @block.sync
            def _(sp):
                sync_program(sp, main, True)

            @block.gpsimd
            def _(pool):
                pool.memset(ident[:, :], 0.0).then_inc(constants, 1)
                pool.memset(masker[:, :], 0.0).then_inc(constants, 1)
                pool.memset(spread[:, :], 1.0 / SPREAD).then_inc(constants, 1)
                pool.memset(minus_half[:, :], -0.5).then_inc(constants, 1)
                pool.memset(parts[:, :], 0.0).then_inc(constants, 1)
                pool.wait_ge(constants, 2)
                for m, fill in ((ident, 1.0), (masker, MASKED)):
                    pool.affine_select(out=m[:, :], in_=m[:, :], compare_op=ALU.not_equal, fill=fill, base=0,
                                       pattern=[[-1, 128]], channel_multiplier=1).then_inc(constants, 1)
                pool.wait_ge(constants, CONSTANTS)
                pool_program(pool, main)

            @block.scalar
            def _(act):
                act.dma_start(rows[:, 0:D], t["L0_gnn_b_loop"].to_broadcast([128, D])).then_inc(rows_in, 16)
                act.dma_start(rows[:, D:2 * D], t["L0_gnn_bg_loop"].to_broadcast([128, D])).then_inc(rows_in, 16)
                act.dma_start(rows[:, 2 * D:3 * D], t["L1_gnn_W_b"].unsqueeze(0).to_broadcast([128, D]))\
                   .then_inc(rows_in, 16)
                act.wait_ge(constants, 4)
                nc.scalar.activation(unused[:, :], minus_half[:, :], ACT.Tanh)
                act.wait_ge(turned, 1)
                nc.scalar.activation(WgT[:, :], b_e[:, D:2 * D], ACT.Copy).then_inc(gates_folded, 1)
                nc.scalar.activation(w_hg[:, 0:D], b_e[:, 0:D], ACT.Copy, scale=0.5)
                act.wait_ge(turned, 2)
                nc.scalar.activation(w_hg[:, D:2 * D], b_agg[:, 0:D], ACT.Copy).then_inc(gates_folded, 1)
                start_counts(act, main, "p", "att", "pT")

                relu_first(act, main, 0, 0)
                gate_tanh(act, main, 0, 0)
                act.wait_ge(turned, 4)
                nc.scalar.activation(A[:, :], b_pv[:, 0:D], ACT.Copy)
                nc.scalar.activation(C[:, :], b_pv[:, 2 * D:3 * D], ACT.Copy)
                nc.scalar.activation(a_col[:, :], b_pv[:, D:D + 1], ACT.Identity, bias=qk_b[:, 0:1])
                nc.scalar.activation(c_col[:, :], b_pv[:, 3 * D:3 * D + 1], ACT.Identity, bias=qk_b[:, 1:2])\
                    .then_inc(scores_folded, 1)
                relu_first(act, main, 0, 1)
                act.wait_ge(turned, 5)
                nc.scalar.activation(rows[:, 3 * D:3 * D + 1], b_pv[:, D + 2:D + 3], ACT.Copy,
                                     scale=SCALE * (1.0 - SLOPE)).then_inc(scores_folded, 1)
                nc.scalar.activation(w_v[:, :], b_pv[:, 0:D], ACT.Copy, scale=SCALE)
                nc.scalar.activation(v_bias[:, :], b_pv[:, D:D + 1], ACT.Copy, scale=SCALE)
                nc.scalar.activation(w_hw[:, D:D + 1], b_pv[:, D + 1:D + 2], ACT.Copy,
                                     scale=SCALE * (1.0 - SLOPE)).then_inc(scores_folded, 1)
                gate_tanh(act, main, 0, 1)
                s = slice(3 * D, 3 * D + 1)
                act.wait_ge(scores_folded, 3)
                nc.scalar.activation(high[:, s], rows[:, s], ACT.Copy).then_inc(scores_folded, 1)
                act.wait_ge(scores_folded, 4)
                nc.scalar.activation(rest[:, s], high[:, s], ACT.Identity, bias=rows[:, s], scale=-1.0)\
                    .then_inc(scores_folded, 1)
                act.wait_ge(scores_folded, 5)
                nc.scalar.activation(middle[:, s], rest[:, s], ACT.Copy).then_inc(scores_folded, 1)
                act.wait_ge(constants, CONSTANTS)
                act.wait_ge(scores_folded, 6)
                nc.scalar.activation(parts[0:32, s], high[0:32, s], ACT.Copy)
                nc.scalar.activation(parts[32:64, s], middle[32:64, s], ACT.Copy)
                nc.scalar.activation(parts[64:96, s], middle[64:96, s], ACT.Identity, bias=rest[64:96, s],
                                     scale=-1.0).then_inc(scores_folded, 1)
                slots(act, lambda j, c: scalar_slot(act, main, j, c), -3, 1, first=1)

            @block.vector
            def _(dve):
                start_counts(dve, main, "rinv", "logits")
                first_norm_stats(dve, main, 0, 0)
                s = slice(0, 3 * D)
                dve.wait_ge(rows_in, 48)
                nc.vector.tensor_scalar(rows[:, 0:D], rows[:, 0:D], 0.5, None, ALU.mult).then_inc(folded, 1)
                dve.wait_ge(folded, 1)
                nc.vector.tensor_copy(high[:, s], rows[:, s]).then_inc(folded, 1)
                dve.wait_ge(folded, 2)
                nc.vector.tensor_tensor(rest[:, s], rows[:, s], high[:, s], ALU.subtract).then_inc(folded, 1)
                dve.wait_ge(folded, 3)
                nc.vector.tensor_copy(middle[:, s], rest[:, s]).then_inc(folded, 1)
                first_norm(dve, main, 0, 0)
                dve.wait_ge(constants, CONSTANTS)
                dve.wait_ge(folded, 4)
                nc.vector.tensor_copy(parts[0:32, s], high[0:32, s])
                nc.vector.tensor_copy(parts[32:64, s], middle[32:64, s])
                nc.vector.tensor_tensor(parts[64:96, s], rest[64:96, s], middle[64:96, s], ALU.subtract)\
                    .then_inc(folded, 1)
                first_norm_stats(dve, main, 0, 1)
                dve.wait_ge(turned, 3)
                nc.vector.tensor_copy(w_hw[:, 0:D], b_pv[:, 0:D])
                nc.vector.tensor_copy(QwT[:, :], b_pv[:, D:2 * D])
                nc.vector.tensor_copy(KwT[:, :], b_pv[:, 2 * D:3 * D]).then_inc(folded, 1)
                first_norm(dve, main, 0, 1)

                def run(j, c):
                    vector_slot(dve, main, j, c)
                    if ends(j, c, 2):
                        dve.wait_ge(main["counted"], GROUPS)
                        nc.vector.tensor_scalar(over[:, :], counted[:, :], PLAIN_SUM + 1.0, None, ALU.is_gt)\
                            .then_inc(flagged, 1)
                        dve.wait_ge(flagged, 1)
                        nc.vector.tensor_reduce(over_row[:, :], over[:, :], AX.X, ALU.max).then_inc(flagged, 1)
                slots(dve, run, -2, 2, first=0)
                dve.wait_ge(flag_turned, 1)
                nc.vector.tensor_reduce(flag[:, :], b_agg[0:1, 0:128], AX.X, ALU.max).then_inc(flagged, 1)

            @block.tensor
            def _(pe):
                start_counts(pe, main, "p_turned", "pv", "scores")
                pe.wait_ge(constants, 4)
                keep_busy(9)
                pe.wait_ge(constants, CONSTANTS)
                pe.wait_ge(weights_in, 32)
                nc.tensor.transpose(b_e[:, 0:D], W_loop[:, :], ident[:, :])
                nc.tensor.transpose(b_e[:, D:2 * D], Wg_loop[:, :], ident[:, :]).then_inc(turned, 1)
                keep_busy(3)
                pe.wait_ge(gates_folded, 1)
                nc.tensor.matmul(b_agg[:, 0:D], W_loop[:, :], WgT[:, :], start=True, stop=True).then_inc(turned, 1)
                keep_busy(2)
                turn_first_norm(pe, main, 0, 0)
                pe.wait_ge(products_in, 48)
                nc.tensor.transpose(b_pv[:, 0:D], W_wb[:, 0:D], ident[:, :])
                nc.tensor.transpose(b_pv[:, D:2 * D], Q_w[:, :], ident[:, :])
                nc.tensor.transpose(b_pv[:, 2 * D:3 * D], K_w[:, :], ident[:, :]).then_inc(turned, 1)
                pe.wait_ge(gates_folded, 2)
                pe.wait_ge(folded, 5)
                gates_products(pe, main, 0, 0)
                pe.wait_ge(folded, 6)
                pe.wait_ge(scores_in, 48)
                nc.tensor.matmul(b_pv[:, 0:D + 1], QwT[:, :], W_wb[:, :], start=True, stop=True)
                nc.tensor.matmul(b_pv[:, 2 * D:3 * D + 1], KwT[:, :], W_wb[:, :], start=True, stop=True)\
                  .then_inc(turned, 1)
                turn_first_norm(pe, main, 0, 1)
                relational_sum(pe, main, 0, 0)
                pe.wait_ge(scores_folded, 1)
                nc.tensor.matmul(b_pv[:, 0:D], A[:, :], C[:, :], start=True, stop=True)
                nc.tensor.matmul(b_pv[:, D:D + 1], C[:, :], a_col[:, :], start=True, stop=True)
                nc.tensor.matmul(b_pv[:, D + 1:D + 2], A[:, :], c_col[:, :], start=True, stop=True)
                nc.tensor.matmul(b_pv[:, D + 2:D + 3], a_col[:, 0:1].to_broadcast([128, 128]), c_col[:, :],
                                 start=True, stop=True).then_inc(turned, 1)

                gates_products(pe, main, 0, 1)
                turn_first_norm(pe, main, 0, 2)
                pe.wait_ge(scores_folded, 7)
                slots(pe, lambda j, c: tensor_slot(pe, main, j, c), -2, 2, first=1)
                pe.wait_ge(flagged, 2)
                pe.wait_ge(main["x1"], GROUPS)
                nc.tensor.transpose(b_agg[0:1, 0:128], over_row[:, :], ident[:, :]).then_inc(flag_turned, 1)


        again = semaphores(sem, "a")
        rel_in = sem("rel_in")
        rel_turned = sem("rel_turned")
        rel_folded = sem("rel_folded")
        gx_in = sem("gx_in")
        gadj_in = sem("gadj_in")
        g_bn = sem("g_bn")
        g_stats = sem("g_stats")
        g_var = sem("g_var")
        g_rstd = sem("g_rstd")
        g_xn = sem("g_xn")
        g_turned = sem("g_turned")
        g_hT = sem("g_hT")
        g_hg = sem("g_hg")
        g_ready = sem("g_ready")
        r_gate_in = sem("r_gate_in")
        r_gate = sem("r_gate")
        r_hot = sem("r_hot")
        r_vals = sem("r_vals")
        r_next = sem("r_next")
        r_summed = sem("r_summed")
        g_sum = sem("g_sum")
        g_extra = sem("g_extra")

        def on_flag(engine, program):
            with engine.If(engine.value_load(flag[0:1, 0:1]) > 0):
                program(engine)
                engine.sem_inc(passed, 1)

        def relation_loads(sp, i):
            sp.dma_start(gx[:, :], t["x"][i]).then_inc(gx_in, 16)
            sp.dma_start(gadj[:, :], t["adj"][i]).then_inc(gadj_in, 16)

        def sync_again(sp):
            for k, name in enumerate(("L0_gnn_W_fwd", "L0_gnn_W_bwd", "L0_gnn_Wg_fwd", "L0_gnn_Wg_bwd")):
                sp.dma_start(rel_natural[:, k * D:(k + 1) * D], t[name]).then_inc(rel_in, 16)
            for k, way in enumerate(("fwd", "bwd")):
                for tile, name in ((rel_b, "b"), (rel_bg, "bg")):
                    row = t[f"L0_gnn_{name}_{way}"].unsqueeze(0).to_broadcast([128, RELS, D])
                    sp.dma_start(tile[:, :, k * D:(k + 1) * D], row).then_inc(rel_in, 16)
            relation_loads(sp, 0)
            with sp.Fori(1, B, 1) as i:
                sp.wait_ge(g_xn, i)
                relation_loads(sp, i)
            sp.wait_ge(g_extra, B)
            sync_program(sp, again)

        def pool_again(pool):
            with pool.Fori(0, B, 1) as i:
                pool.wait_ge(g_stats, i + 1)
                pool.sem_inc(passed, 1)
                pool.tensor_scalar(gvar[:, :], gmv[:, 1:2], EPS, None, ALU.add).then_inc(g_var, 1)
                pool.wait_ge(g_var, i + 1)
                pool.tensor_tensor(grstd[:, :], gvar[:, :], minus_half[:, 0:1], ALU.pow).then_inc(g_rstd, 1)
            pool_program(pool, again)

        def scalar_again(act):
            with act.Fori(0, B, 1) as i:
                with act.Fori(0, RELS, 1) as r:
                    act.wait_ge(r_gate_in, i * RELS + r + 1)
                    nc.scalar.activation(gate[:, :], gate_in[:, :], ACT.Tanh, scale=0.5).then_inc(r_gate, 1)
            start_counts(act, again, "p", "att", "pT")
            slots(act, lambda j, c: scalar_slot(act, again, j, c), -3, 1)

        def vector_again(dve):
            nc.vector.memset(zeros[:, :], 0.0).then_inc(rel_folded, 1)
            dve.wait_ge(rel_turned, 1)
            nc.vector.tensor_copy(rel_WgT[:, :], b_e[:, 2 * D:4 * D]).then_inc(rel_folded, 1)
            nc.vector.tensor_copy(rel_w[:, 0:2 * D], b_e[:, 0:2 * D]).then_inc(rel_folded, 1)
            dve.wait_ge(rel_turned, 2)
            nc.vector.tensor_copy(rel_w[:, 2 * D:4 * D], b_pv[:, 0:2 * D]).then_inc(rel_folded, 1)
            dve.wait_ge(rel_in, 16 * 8)
            with dve.Fori(0, B, 1) as i:
                dve.wait_ge(gx_in, i * 16 + 16)
                nc.vector.bn_stats(gbn[:, :], gx[:, :]).then_inc(g_bn, 1)
                dve.wait_ge(g_bn, i + 1)
                dve.sem_inc(passed, 1)
                nc.vector.bn_aggr(gmv[:, :], gbn[:, :]).then_inc(g_stats, 1)
                dve.wait_ge(gadj_in, i * 16 + 16)
                nc.vector.tensor_copy(adj_both[:, D:2 * D], gadj[:, :])
                dve.wait_ge(g_rstd, i + 1)
                nc.vector.tensor_scalar(gxn[:, :], gx[:, :], gmv[:, 0:1], grstd[:, 0:1], ALU.subtract, ALU.mult)\
                    .then_inc(g_xn, 1)
                dve.wait_ge(g_turned, i + 1)
                nc.vector.tensor_scalar(ghT[:, :], b_h1[:, 0:D], 0.0, None, ALU.max)
                nc.vector.tensor_copy(adj_both[:, 0:D], b_h1[:, D:2 * D]).then_inc(g_hT, 1)
                dve.wait_ge(g_hg, i + 1)
                nc.vector.memset(relation[:, :], 2.0)
                nc.vector.tensor_copy(ghg[:, :], b_hg[:, 0:4 * D]).then_inc(g_ready, 1)
                dve.wait_ge(g_ready, i + 1)
                dve.sem_inc(passed, 1)
                with dve.Fori(0, RELS, 1) as r:
                    done = i * RELS + r
                    nc.vector.tensor_tensor(gate_in[:, :], ghg[:, 2 * D:4 * D], rel_bg[:, bass.ds(r, 1), :], ALU.add)\
                        .then_inc(r_gate_in, 1)
                    dve.wait_ge(r_summed, done + 1)
                    nc.vector.tensor_tensor(lifted[:, :], ghg[:, 0:2 * D], rel_b[:, bass.ds(r, 1), :], ALU.add)
                    nc.vector.tensor_scalar(half_hot[:, :], adj_both[:, :], relation[:, 0:1], 0.5, ALU.is_equal,
                                            ALU.mult).then_inc(r_hot, 1)
                    dve.wait_ge(r_hot, done + 1)
                    nc.vector.tensor_scalar(relation[:, :], relation[:, :], 1.0, None, ALU.add).then_inc(r_next, 1)
                    dve.wait_ge(r_gate, done + 1)
                    nc.vector.scalar_tensor_tensor(gvals[:, :], gate[:, :], 1.0, lifted[:, :], ALU.add, ALU.mult)\
                        .then_inc(r_vals, 1)
                    dve.wait_ge(r_next, done + 1)
                dve.wait_ge(g_sum, i + 1)
                nc.vector.tensor_copy(extra[:, bass.ds(i * D, D)], b_agg[:, 0:D]).then_inc(g_extra, 1)
            dve.wait_ge(g_extra, B)
            start_counts(dve, again, "rinv", "logits")
            slots(dve, lambda j, c: vector_slot(dve, again, j, c, extra), -2, 2)

        def tensor_again(pe):
            pe.sem_inc(r_summed, 1)
            pe.wait_ge(rel_in, 16 * 8)
            for k in range(4):
                ins = nc.tensor.transpose(b_e[:, k * D:(k + 1) * D], rel_natural[:, k * D:(k + 1) * D], ident[:, :])
            ins.then_inc(rel_turned, 1)
            pe.wait_ge(rel_folded, 2)
            for k in range(2):
                ins = nc.tensor.matmul(b_pv[:, k * D:(k + 1) * D], rel_natural[:, k * D:(k + 1) * D],
                                       rel_WgT[:, k * D:(k + 1) * D], start=True, stop=True)
            ins.then_inc(rel_turned, 1)
            pe.wait_ge(rel_folded, 4)
            with pe.Fori(0, B, 1) as i:
                pe.wait_ge(g_xn, i + 1)
                nc.tensor.transpose(b_h1[:, 0:D], gxn[:, :], ident[:, :])
                nc.tensor.transpose(b_h1[:, D:2 * D], adj_both[:, D:2 * D], ident[:, :]).then_inc(g_turned, 1)
                pe.wait_ge(g_hT, i + 1)
                nc.tensor.matmul(b_hg[:, 0:4 * D], ghT[:, :], rel_w[:, :], start=True, stop=True).then_inc(g_hg, 1)
                nc.tensor.matmul(b_agg[:, 0:D], zeros[:, :], zeros[:, :], start=True, stop=False)
                with pe.Fori(0, RELS, 1) as r:
                    pe.wait_ge(r_vals, i * RELS + r + 1)
                    for k in range(2):
                        ins = nc.tensor.matmul(b_agg[:, 0:D], half_hot[:, k * D:(k + 1) * D],
                                               gvals[:, k * D:(k + 1) * D], start=False, stop=False)
                    ins.then_inc(r_summed, 1)
                nc.tensor.matmul(b_agg[:, 0:D], zeros[:, :], zeros[:, :], start=False, stop=True).then_inc(g_sum, 1)
            start_counts(pe, again, "p_turned", "pv", "scores")
            slots(pe, lambda j, c: tensor_slot(pe, again, j, c), -2, 2)

        with nc.Block() as block:
            @block.sync
            def _(sp):
                on_flag(sp, sync_again)

            @block.gpsimd
            def _(pool):
                on_flag(pool, pool_again)

            @block.scalar
            def _(act):
                on_flag(act, scalar_again)

            @block.vector
            def _(dve):
                on_flag(dve, vector_again)

            @block.tensor
            def _(pe):
                on_flag(pe, tensor_again)


_INS = ['x', 'adj', 'L0_gnn_W_fwd', 'L0_gnn_W_bwd', 'L0_gnn_W_loop', 'L0_gnn_Wg_fwd', 'L0_gnn_Wg_bwd',
        'L0_gnn_Wg_loop', 'L0_gnn_b_fwd', 'L0_gnn_b_bwd', 'L0_gnn_b_loop', 'L0_gnn_bg_fwd', 'L0_gnn_bg_bwd',
        'L0_gnn_bg_loop', 'L1_gnn_W_w', 'L1_gnn_W_b', 'L1_gnn_Q_w', 'L1_gnn_Q_b', 'L1_gnn_K_w', 'L1_gnn_K_b']


def kernel(**inputs):
    import numpy as _np
    import concourse.bacc as _bacc
    from concourse import mybir as _mybir
    from concourse.bass_utils import run_bass_kernel_spmd as _run

    nc = _bacc.Bacc("TRN2", target_bir_lowering=False, num_devices=1)
    arrays, aps = {}, {}
    for name in _INS:
        arrays[f"in_{name}"] = _np.ascontiguousarray(inputs[name])
        a = arrays[f"in_{name}"]
        aps[name] = nc.dram_tensor(f"in_{name}", a.shape, _mybir.dt.from_np(a.dtype), kind="ExternalInput").ap()
    out = nc.dram_tensor("out", (B, N, D), F32, kind="ExternalOutput").ap()
    build(nc, aps, out)
    r = _run(nc, [arrays], core_ids=[0])
    return r.results[0]["out"]
```
